# Optimizing a Trainium2 kernel written in Bass

```python
import numpy as np
import jax
import jax.numpy as jnp

def _softmax(x, axis=-1):
    return jax.nn.softmax(x, axis=axis)

def _gelu(x):
    return jax.nn.gelu(x, approximate=True)

def _silu(x):
    return jax.nn.silu(x)

def _sigmoid(x):
    return jax.nn.sigmoid(x)

def _layernorm(x, axis=-1, eps=1e-05):
    m = jnp.mean(x, axis=axis, keepdims=True)
    v = jnp.var(x, axis=axis, keepdims=True)
    return (x - m) / jnp.sqrt(v + eps)

def _scatter_add(tgt, idx, src, axis=0):
    return tgt.at[idx].add(src)

def _segment_sum(src, seg, n):
    return jax.ops.segment_sum(src, seg, n)
kernel_name = 'mk_macaron_d1_jaxref_r4_a2a419'

def setup_inputs(seed: int=0):
    np.random.seed(seed)
    _w = jnp.asarray

    def _L0_attn_setup():
        import jax, jax.numpy as jnp
        import numpy as np
        D_MODEL = 256
        N_HEADS = 16
        HEAD_DIM = D_MODEL // N_HEADS
        ROPE_THETA = 10000.0

        def _rope_cache(seq_len, head_dim, dtype, theta=ROPE_THETA):
            half = head_dim // 2
            inv_freq = 1.0 / theta ** (jnp.arange(half, dtype=jnp.float32) / half)
            t = jnp.arange(seq_len, dtype=jnp.float32)
            freqs = jnp.outer(t, inv_freq)
            emb = jnp.concatenate([freqs, freqs], axis=-1)
            return (jnp.cos(emb).astype(dtype), jnp.sin(emb).astype(dtype))

        def _rotate_half(x):
            d = x.shape[-1]
            x1, x2 = (x[..., :d // 2], x[..., d // 2:])
            return jnp.concatenate([-x2, x1], axis=-1)

        def _apply_rope(x, cos, sin):
            return x * cos + _rotate_half(x) * sin
        key = jax.random.key(seed)
        ks = jax.random.split(key, 9)
        B, L, D = (2, 512, D_MODEL)
        s = 1.0 / np.sqrt(D)
        return {'x': jax.random.normal(ks[0], (B, L, D), dtype=jnp.float32), 'Wq': jax.random.normal(ks[1], (D, D), dtype=jnp.float32) * s, 'bq': jnp.zeros((D,), dtype=jnp.float32), 'Wk': jax.random.normal(ks[2], (D, D), dtype=jnp.float32) * s, 'bk': jnp.zeros((D,), dtype=jnp.float32), 'Wv': jax.random.normal(ks[3], (D, D), dtype=jnp.float32) * s, 'bv': jnp.zeros((D,), dtype=jnp.float32), 'Wo': jax.random.normal(ks[4], (D, D), dtype=jnp.float32) * s, 'bo': jnp.zeros((D,), dtype=jnp.float32)}
    _L0_attn_in = _L0_attn_setup()

    def _L0_ffn_setup():
        import jax, jax.numpy as jnp
        import numpy as np
        NUM_EXPERTS = 8
        TOP_K = 2
        key = jax.random.key(seed)
        ks = jax.random.split(key, 4)
        B, S, H, F = (4, 1024, 256, 1024)
        x = jax.random.normal(ks[0], (B, S, H), dtype=jnp.float32)
        router_w = jax.random.normal(ks[1], (H, NUM_EXPERTS), dtype=jnp.float32) * 0.02
        w1 = jax.random.normal(ks[2], (H, F), dtype=jnp.float32) * 0.02
        b1 = jnp.zeros((F,), dtype=jnp.float32)
        w2 = jax.random.normal(ks[3], (F, H), dtype=jnp.float32) * 0.02
        b2 = jnp.zeros((H,), dtype=jnp.float32)
        return {'x': x, 'router_w': router_w, 'w1': w1, 'b1': b1, 'w2': w2, 'b2': b2}
    _L0_ffn_in = _L0_ffn_setup()
    _d = {'L0_attn_x': _L0_attn_in['x'], 'L0_attn_Wq': _L0_attn_in['Wq'], 'L0_attn_bq': _L0_attn_in['bq'], 'L0_attn_Wk': _L0_attn_in['Wk'], 'L0_attn_bk': _L0_attn_in['bk'], 'L0_attn_Wv': _L0_attn_in['Wv'], 'L0_attn_bv': _L0_attn_in['bv'], 'L0_attn_Wo': _L0_attn_in['Wo'], 'L0_attn_bo': _L0_attn_in['bo'], 'L0_ffn_router_w': _L0_ffn_in['router_w'], 'L0_ffn_w1': _L0_ffn_in['w1'], 'L0_ffn_b1': _L0_ffn_in['b1'], 'L0_ffn_w2': _L0_ffn_in['w2'], 'L0_ffn_b2': _L0_ffn_in['b2']}
    _x0 = _d['L0_attn_x']
    _d['L0_attn_x'] = jax.random.normal(jax.random.fold_in(jax.random.key(seed), 1), (4, 2048, 256), dtype=_x0.dtype)
    del _x0
    return _d

def reference(L0_attn_x, L0_attn_Wq, L0_attn_bq, L0_attn_Wk, L0_attn_bk, L0_attn_Wv, L0_attn_bv, L0_attn_Wo, L0_attn_bo, L0_ffn_router_w, L0_ffn_w1, L0_ffn_b1, L0_ffn_w2, L0_ffn_b2):

    def _L0_attn_ref(x, Wq, bq, Wk, bk, Wv, bv, Wo, bo):
        import jax, jax.numpy as jnp
        import numpy as np
        D_MODEL = 256
        N_HEADS = 16
        HEAD_DIM = D_MODEL // N_HEADS
        ROPE_THETA = 10000.0

        def _rope_cache(seq_len, head_dim, dtype, theta=ROPE_THETA):
            half = head_dim // 2
            inv_freq = 1.0 / theta ** (jnp.arange(half, dtype=jnp.float32) / half)
            t = jnp.arange(seq_len, dtype=jnp.float32)
            freqs = jnp.outer(t, inv_freq)
            emb = jnp.concatenate([freqs, freqs], axis=-1)
            return (jnp.cos(emb).astype(dtype), jnp.sin(emb).astype(dtype))

        def _rotate_half(x):
            d = x.shape[-1]
            x1, x2 = (x[..., :d // 2], x[..., d // 2:])
            return jnp.concatenate([-x2, x1], axis=-1)

        def _apply_rope(x, cos, sin):
            return x * cos + _rotate_half(x) * sin
        B, L, D = x.shape
        H, Hd = (N_HEADS, HEAD_DIM)
        scale = Hd ** (-0.5)

        def proj(W, b):
            return (x @ W.T + b).reshape(B, L, H, Hd).transpose(0, 2, 1, 3)
        q = proj(Wq, bq)
        k = proj(Wk, bk)
        v = proj(Wv, bv)
        cos, sin = _rope_cache(L, Hd, x.dtype)
        q = _apply_rope(q, cos, sin)
        k = _apply_rope(k, cos, sin)
        scores = jnp.einsum('bhqd,bhkd->bhqk', q, k) * scale
        attn = jax.nn.softmax(scores, axis=-1)
        ctx = jnp.einsum('bhqk,bhkd->bhqd', attn, v)
        ctx = ctx.transpose(0, 2, 1, 3).reshape(B, L, D)
        return ctx @ Wo.T + bo

    def _L0_ffn_ref(x, router_w, w1, b1, w2, b2):
        import jax, jax.numpy as jnp
        import numpy as np
        NUM_EXPERTS = 8
        TOP_K = 2
        B, S, H = x.shape
        xt = x.reshape(-1, H)
        router_logits = jnp.matmul(xt, router_w)
        router_probs = jax.nn.softmax(router_logits, axis=-1)
        top_k_probs, top_k_indices = jax.lax.top_k(router_probs, TOP_K)
        top_k_probs = top_k_probs / jnp.sum(top_k_probs, axis=-1, keepdims=True)
        one_hot = jax.nn.one_hot(top_k_indices, NUM_EXPERTS, dtype=xt.dtype)
        combine = jnp.einsum('tk,tke->te', top_k_probs, one_hot)
        expert_out = jnp.matmul(jax.nn.gelu(jnp.matmul(xt, w1) + b1), w2) + b2
        out = expert_out * jnp.sum(combine, axis=-1, keepdims=True)
        return out.reshape(B, S, H)
    x = L0_attn_x
    x = x + 0.5 * _L0_ffn_ref(_layernorm(x, axis=-1), L0_ffn_router_w, L0_ffn_w1, L0_ffn_b1, L0_ffn_w2, L0_ffn_b2)
    x = x + _L0_attn_ref(_layernorm(x, axis=-1), L0_attn_Wq, L0_attn_bq, L0_attn_Wk, L0_attn_bk, L0_attn_Wv, L0_attn_bv, L0_attn_Wo, L0_attn_bo)
    x = x + 0.5 * _L0_ffn_ref(_layernorm(x, axis=-1), L0_ffn_router_w, L0_ffn_w1, L0_ffn_b1, L0_ffn_w2, L0_ffn_b2)
    return x

_drawn_inputs = setup_inputs


def setup_inputs(seed=0):
    import zlib

    import numpy as np

    out = dict(_drawn_inputs(seed))
    spreads = {'L0_attn_bq': (0.0, 0.8),
     'L0_attn_bk': (0.0, 0.8),
     'L0_attn_bv': (0.0, 0.1),
     'L0_attn_bo': (0.0, 0.1),
     'L0_ffn_b1': (0.0, 0.1),
     'L0_ffn_b2': (0.0, 0.1)}
    factors = {'L0_ffn_router_w': 8.0}
    for name, (base, spread) in spreads.items():
        noise = np.random.default_rng([zlib.crc32(name.encode()), seed]).standard_normal(out[name].shape)
        drawn = base * np.exp(spread * noise) if base else spread * noise
        out[name] = jnp.asarray(drawn.astype(out[name].dtype))
    for name, factor in factors.items():
        out[name] = (out[name] * factor).astype(out[name].dtype)
    return out
```

```python
from contextlib import ExitStack

import concourse.bass as bass
from concourse import mybir

ALU = mybir.AluOpType
ACT = mybir.ActivationFunctionType
F32 = mybir.dt.float32
BF16 = mybir.dt.bfloat16
X = mybir.AxisListType.X

P = 128
BATCH, SEQ, D = 4, 2048, 256
HEADS, HD = 16, 16
FF, EXPERTS, TOP_K = 1024, 8, 2
TOKENS = BATCH * SEQ
EPS = 1e-5

KD = D // P
FB = FF // P
CH = 512
TT = CH // P
CHUNKS = TOKENS // CH

QUAD = 4
GROUPS = BATCH * HEADS // QUAD
QC = SEQ // CH
KB = SEQ // P
VW = 32
PARTS = 3
Q_PART = (0, 0, 0, 1, 1, 2)
K_PART = (0, 1, 2, 0, 1, 0)
SR = HD * len(Q_PART)
SHIFT_ROW = SR
STACK = SR + PARTS
RING = 3
SCORE_SCALE = HD ** -0.5


def wait(eng, sem, value):
    if not (isinstance(value, int) and value <= 0):
        eng.wait_ge(sem, value)


def build(nc, x, wqkv, bqkv, wo, bo, router, w1, b1, w2, b2, rope, ident, out):
    ctx = ExitStack()
    with ctx:
        x2_dram = nc.dram_tensor("x2_dram", (TOKENS, D), F32, kind="Internal").ap()
        qk_dram = nc.dram_tensor("qk_dram", (GROUPS, PARTS, 2, QUAD * HD, SEQ), BF16, kind="Internal").ap()
        v_dram = nc.dram_tensor("v_dram", (TOKENS, HEADS * VW), F32, kind="Internal").ap()
        ctx_dram = nc.dram_tensor("ctx_dram", (GROUPS, P, SEQ), F32, kind="Internal").ap()
        with ExitStack() as phase:
            project_phase(nc, phase, x, wqkv, bqkv, router, w1, b1, w2, b2, rope, ident, x2_dram, qk_dram, v_dram)
        with ExitStack() as phase:
            attention_phase(nc, phase, ident, qk_dram, v_dram, ctx_dram)
        with ExitStack() as phase:
            output_phase(nc, phase, wo, bo, router, w1, b1, w2, b2, ident, x2_dram, ctx_dram, out)


def tok_tiles(ap, chunk):
    return ap[bass.ds(chunk * CH, CH), :].rearrange("(t p) n -> p t n", p=P)



def ffn_buffers(nc, phase, pre):
    def sb(name, shape, dt=F32):
        return phase.enter_context(nc.sbuf_tensor(pre + name, shape, dt))

    def sem(name):
        return phase.enter_context(nc.semaphore(pre + name))

    f = Buffers()
    f.w1 = sb("w1", [P, KD, FF])
    f.w2 = sb("w2", [P, FB, D])
    f.router = sb("router", [P, KD, EXPERTS])
    f.b1 = sb("b1", [P, FB])
    f.b2 = sb("b2", [P, D])
    f.ident = sb("ident", [P, P])
    f.consts = sb("consts", [P, 4, TT])
    f.x_in = sb("x_in", [P, TT, D])
    f.x_res = sb("x_res", [P, TT, D])
    f.xn = sb("xn", [P, TT, D])
    f.xnT = sb("xnT", [P, KD, CH])
    f.hT = sb("hT", [P, FB, CH])
    f.ffn_out = sb("ffn_out", [P, TT, D])
    f.y = sb("y", [P, TT, D])
    f.top = sb("top", [P, TT, EXPERTS])
    f.top_max = sb("top_max", [P, TT])
    f.top_shift = sb("top_shift", [P, TT, EXPERTS])
    f.top_exp = sb("top_exp", [P, TT, EXPERTS])
    f.exp_sum = sb("exp_sum", [P, TT])
    f.exp_rec = sb("exp_rec", [P, TT])
    f.top_prob = sb("top_prob", [P, TT, TOP_K])
    f.top_sum = sb("top_sum", [P, TT])
    f.top_rec = sb("top_rec", [P, TT])
    f.combine = sb("combine", [P, TT, TOP_K])
    f.gate = sb("gate", [P, TT])
    f.gate_half = sb("gate_half", [P, TT])
    f.banks = phase.enter_context(nc.psum_tensor(pre + "banks", [P, 8, CH], F32))
    f.tr = [f.banks[:, k, :] for k in range(2)]
    f.up = [f.banks[:, 2 + k, :] for k in range(2)]
    f.down = [f.banks[:, 4 + k, 0:D] for k in range(2)]
    f.logits = f.banks[:, 0, 0:TT * EXPERTS].rearrange("p (t e) -> p t e", e=EXPERTS)
    f.weights_s = sem("weights")
    f.x_loaded_s = sem("x_loaded")
    f.res_loaded_s = sem("res_loaded")
    f.res_copied_s = sem("res_copied")
    f.xn_t_s = sem("xn_t")
    f.xn_taken_s = sem("xn_taken")
    f.up_s = sem("up")
    f.gelu_s = sem("gelu")
    f.down_s = sem("down")
    f.logits_s = sem("logits")
    f.top_s = sem("top")
    f.top_max_s = sem("top_max")
    f.shifted_s = sem("shifted")
    f.exped_s = sem("exped")
    f.gate_step_s = sem("gate_step")
    f.half_s = sem("half")
    f.ffn_sum_s = sem("ffn_sum")
    f.y_ready_s = sem("y_ready")
    f.ln1 = norm_buffers(nc, phase, pre + "ln1_")
    return f


class Buffers:
    pass


def norm_buffers(nc, phase, pre):
    def sb(name, shape):
        return phase.enter_context(nc.sbuf_tensor(pre + name, shape, F32))

    n = Buffers()
    n.stats = sb("stats", [P, TT, 6])
    n.moments = sb("moments", [P, TT, 2])
    n.fence = sb("fence", [P, 1])
    n.var = sb("var", [P, TT])
    n.guess = sb("guess", [P, TT])
    n.square = sb("square", [P, TT])
    n.product = sb("product", [P, TT])
    n.half = sb("half", [P, TT])
    n.factor = sb("factor", [P, TT])
    n.rstd = sb("rstd", [P, TT])
    def sem(name):
        return phase.enter_context(nc.semaphore(pre + name))

    n.stats_s = sem("stats_s")
    n.moments_s = sem("moments_s")
    n.root_step_s = sem("root_step_s")
    n.rstd_s = sem("rstd_s")
    n.normed_s = sem("normed_s")
    return n


def load_ffn_weights(eng, f, router, w1, b1, w2, b2, ident):
    eng.dma_start(f.ident[:, :], ident).then_inc(f.weights_s, 16)
    eng.dma_start(f.router[:, :, :], router.rearrange("(k p) e -> p k e", p=P)).then_inc(f.weights_s, 16)
    eng.dma_start(f.w1[:, :, :], w1.rearrange("(k p) n -> p k n", p=P)).then_inc(f.weights_s, 16)
    eng.dma_start(f.b1[:, :], b1).then_inc(f.weights_s, 16)
    eng.dma_start(f.w2[:, :, :], w2.rearrange("(k p) n -> p k n", p=P)).then_inc(f.weights_s, 16)
    eng.dma_start(f.b2[:, :], b2.partition_broadcast(P)).then_inc(f.weights_s, 16)


FFN_WEIGHTS = 6 * 16


def norm_tile_stats(dve, n, src, t):
    dve.bn_stats(n.stats[:, t, :], src[:, t, :]).then_inc(n.stats_s, 1)


def norm_moments(dve, n, i):
    dve.wait_ge(n.stats_s, (i + 1) * TT)
    dve.tensor_copy(n.fence[:, :], n.stats[:, TT - 1, 0:1])
    for t in range(TT):
        dve.bn_aggr(n.moments[:, t, :], n.stats[:, t, :]).then_inc(n.moments_s, 1)


def norm_apply(dve, n, src, dst, i):
    dve.wait_ge(n.rstd_s, i + 1)
    for t in range(TT):
        dve.tensor_scalar(dst[:, t, :], src[:, t, :], n.moments[:, t, 0:1], n.rstd[:, t:t + 1],
                          ALU.subtract, ALU.mult).then_inc(n.normed_s, 1)


ROOT_STEPS = 6


def norm_constants(pool, f, consts_s):
    for k, value in enumerate((EPS, -0.5, 1.5, 1.0)):
        pool.memset(f.consts[:, k, :], value).then_inc(consts_s, 1)
    pool.wait_ge(consts_s, 4)


def norm_root(pool, f, n, i):
    eps, minus_half, three_halves = (f.consts[:, k, :] for k in range(3))
    steps = (
        (n.var, n.moments[:, :, 1], eps, ALU.add),
        (n.guess, n.var[:, :], minus_half, ALU.pow),
        (n.square, n.guess[:, :], n.guess[:, :], ALU.mult),
        (n.product, n.square[:, :], n.var[:, :], ALU.mult),
        (n.half, n.product[:, :], minus_half, ALU.mult),
        (n.factor, n.half[:, :], three_halves, ALU.add),
    )
    pool.wait_ge(n.moments_s, i * TT + TT)
    wait(pool, n.normed_s, i * TT)
    for k, (dst, in0, in1, op) in enumerate(steps):
        if k:
            pool.wait_ge(n.root_step_s, i * ROOT_STEPS + k)
        pool.tensor_tensor(dst[:, :], in0, in1, op).then_inc(n.root_step_s, 1)
    pool.wait_ge(n.root_step_s, i * ROOT_STEPS + ROOT_STEPS)
    pool.tensor_tensor(n.rstd[:, :], n.guess[:, :], n.factor[:, :], ALU.mult).then_inc(n.rstd_s, 1)


def transpose_tokens(pe, f, src, tr):
    for k in range(KD):
        for t in range(TT):
            last = pe.transpose(tr[k][:, t * P:(t + 1) * P], src[:, t, k * P:(k + 1) * P], f.ident[:, :])
    return last


def pe_front(pe, f, i, xn_ready):
    pe.wait_ge(f.ln1.normed_s, (i + 1) * TT)
    xn_ready()
    transpose_tokens(pe, f, f.xn, f.tr).then_inc(f.xn_t_s, 1)
    pe.wait_ge(f.xn_taken_s, (i + 1) * KD)
    for t in range(TT):
        for k in range(KD):
            last = pe.matmul(f.logits[:, t, :], f.xnT[:, k, t * P:(t + 1) * P], f.router[:, k, :],
                             start=(k == 0), stop=(k == KD - 1))
    last.then_inc(f.logits_s, 1)
    for b in range(FB):
        wait(pe, f.gelu_s, i * FB + b - 1)
        for k in range(KD):
            last = pe.matmul(f.up[b % 2], f.w1[:, k, b * P:(b + 1) * P], f.xnT[:, k, :],
                             start=(k == 0), stop=(k == KD - 1))
        last.then_inc(f.up_s, 1)


def pe_down(pe, f, i, t):
    if t == 0:
        pe.wait_ge(f.gelu_s, (i + 1) * FB)
    wait(pe, f.ffn_sum_s, i * TT + t - 1)
    for b in range(FB):
        last = pe.matmul(f.down[t % 2], f.hT[:, b, t * P:(t + 1) * P], f.w2[:, b, :],
                         start=(b == 0), stop=(b == FB - 1))
    last.then_inc(f.down_s, 1)


def act_front(act, f, i):
    act.wait_ge(f.xn_t_s, i + 1)
    wait(act, f.up_s, i * FB)
    for k in range(KD):
        act.activation(f.xnT[:, k, :], f.tr[k], ACT.Copy).then_inc(f.xn_taken_s, 1)
    wait(act, f.down_s, i * TT)
    for b in range(FB):
        act.wait_ge(f.up_s, i * FB + b + 1)
        act.activation(f.hT[:, b, :], f.up[b % 2], ACT.Gelu_apprx_tanh, bias=f.b1[:, b:b + 1]).then_inc(f.gelu_s, 1)
    act.wait_ge(f.shifted_s, i + 1)
    act.activation(f.top_exp[:, :, :], f.top_shift[:, :, :], ACT.Exp).then_inc(f.exped_s, 1)


def dve_router(dve, f, i):
    dve.wait_ge(f.logits_s, i + 1)
    dve.reduce_max(f.top_max[:, :], f.logits, axis=X).then_inc(f.top_max_s, 1)
    for t in range(TT):
        dve.max(f.top[:, t, :], f.logits[:, t, :]).then_inc(f.top_s, 1)
    dve.wait_ge(f.top_max_s, i + 1)
    dve.wait_ge(f.top_s, (i + 1) * TT)
    wait(dve, f.exped_s, i)
    dve.tensor_tensor(f.top_shift[:, :, :], f.top[:, :, :], f.top_max[:, :].unsqueeze(2).to_broadcast([P, TT, EXPERTS]),
                      ALU.subtract).then_inc(f.shifted_s, 1)


GATE_STEPS = 7


def dve_gate(dve, f, i):
    s, base = f.gate_step_s, i * GATE_STEPS
    dve.wait_ge(f.exped_s, i + 1)
    dve.reduce_sum(f.exp_sum[:, :], f.top_exp[:, :, :], axis=X).then_inc(s, 1)
    dve.wait_ge(s, base + 1)
    dve.reciprocal(f.exp_rec[:, :], f.exp_sum[:, :]).then_inc(s, 1)
    dve.wait_ge(s, base + 2)
    dve.tensor_tensor(f.top_prob[:, :, :], f.top_exp[:, :, 0:TOP_K],
                      f.exp_rec[:, :].unsqueeze(2).to_broadcast([P, TT, TOP_K]), ALU.mult).then_inc(s, 1)
    dve.wait_ge(s, base + 3)
    dve.reduce_sum(f.top_sum[:, :], f.top_prob[:, :, :], axis=X).then_inc(s, 1)
    dve.wait_ge(s, base + 4)
    dve.reciprocal(f.top_rec[:, :], f.top_sum[:, :]).then_inc(s, 1)
    dve.wait_ge(s, base + 5)
    dve.tensor_tensor(f.combine[:, :, :], f.top_prob[:, :, :],
                      f.top_rec[:, :].unsqueeze(2).to_broadcast([P, TT, TOP_K]), ALU.mult).then_inc(s, 1)
    dve.wait_ge(s, base + 6)
    dve.reduce_sum(f.gate[:, :], f.combine[:, :, :], axis=X).then_inc(s, 1)
    dve.wait_ge(s, base + 7)
    dve.tensor_scalar(f.gate_half[:, :], f.gate[:, :], 0.5, None, ALU.mult).then_inc(f.half_s, 1)
    dve.wait_ge(f.half_s, i + 1)


def dve_residual(dve, f, i, t, res):
    dve.wait_ge(f.down_s, i * TT + t + 1)
    dve.tensor_tensor(f.ffn_out[:, t, :], f.down[t % 2], f.b2[:, :], ALU.add).then_inc(f.ffn_sum_s, 1)
    dve.wait_ge(f.ffn_sum_s, i * TT + t + 1)
    dve.scalar_tensor_tensor(f.y[:, t, :], f.ffn_out[:, t, :], f.gate_half[:, t:t + 1], res[:, t, :],
                             ALU.mult, ALU.add).then_inc(f.y_ready_s, 1)



def project_phase(nc, phase, x, wqkv, bqkv, router, w1, b1, w2, b2, rope, ident, x2_dram, qk_dram, v_dram):
    def sb(name, shape, dt=F32):
        return phase.enter_context(nc.sbuf_tensor("a_" + name, shape, dt))

    def sem(name):
        return phase.enter_context(nc.semaphore("a_" + name))

    f = ffn_buffers(nc, phase, "a_")
    ln2 = norm_buffers(nc, phase, "a_ln2_")
    wqkv_sb = sb("wqkv", [P, KD, 3 * D])
    bqkv_sb = sb("bqkv", [P, 3 * D])
    x2n = sb("x2n", [P, TT, D])
    x2nT = sb("x2nT", [P, KD, CH])
    rope_sb = sb("rope_sb", [P, TT, 2, HD])
    HQK = 2 * HEADS
    qk = sb("qk", [P, 2, HQK, HD])
    qk_cos = sb("qk_cos", [P, HQK, HD])
    qk_sin = sb("qk_sin", [P, HQK, HD])
    qk_rot = sb("qk_rot", [P, 2, HQK * HD])
    rest = sb("rest", [P, 2, 4, P])
    parts = sb("parts", [P, PARTS, 4, CH], BF16)
    v_sb = sb("v_sb", [P, TT, HEADS, VW])
    qk_bank = f.banks[:, 6, :]
    v_bank = f.banks[:, 7, 0:D]

    consts_s = sem("consts")
    rope_loaded_s = sem("rope_loaded")
    x2_t_s = sem("x2_t")
    x2_taken_s = sem("x2_taken")
    qkv_s = sem("qkv")
    qk_biased_s = sem("qk_biased")
    v_biased_s = sem("v_biased")
    rope_step_s = sem("rope_step")
    roped_s = sem("roped")
    roped_t_s = sem("roped_t")
    part0_s = sem("part0")
    rest_s = sem("rest_ready")
    part1_s = sem("part1")
    part2_s = sem("part2")
    x2_out_s = sem("x2_out")
    parts_out_s = sem("parts_out")
    v_out_s = sem("v_out")
    WEIGHTS = FFN_WEIGHTS + 2 * 16
    PARTS_OUT = PARTS * 4 * 2 * 16

    def run(eng, step, back_last):
        step(0, front=True, back=False, more=True)
        step(1, front=True, back=True, more=True)
        with eng.Fori(2, CHUNKS - 1) as i:
            step(i, front=True, back=True, more=True)
        step(CHUNKS - 1, front=True, back=True, more=False)
        if back_last:
            step(CHUNKS, front=False, back=True, more=False)

    with nc.Block() as block:
        @block.sync
        def _(sp):
            sp.dma_start(f.x_in[:, :, :], tok_tiles(x, 0)).then_inc(f.x_loaded_s, 16)
            load_ffn_weights(sp, f, router, w1, b1, w2, b2, ident)
            sp.dma_start(wqkv_sb[:, :, :], wqkv.rearrange("(k p) n -> p k n", p=P)).then_inc(f.weights_s, 16)
            sp.dma_start(bqkv_sb[:, :], bqkv.partition_broadcast(P)).then_inc(f.weights_s, 16)

            def store_back(j):
                sp.wait_ge(part0_s, (j + 1) * TT)
                sp.wait_ge(part1_s, (j + 1) * TT)
                sp.wait_ge(part2_s, (j + 1) * TT)
                batch, at = j // QC, (j % QC) * CH
                for c in range(PARTS):
                    for which in range(2):
                        for half in range(2):
                            for two in range(2):
                                dst = qk_dram[bass.ds(batch * 4 + (2 * half + two), 1), c, which, :, bass.ds(at, CH)]
                                sp.dma_start(dst.rearrange("g p t -> (g p) t"),
                                             parts[64 * two:64 * two + 64, c, 2 * which + half, :]).then_inc(parts_out_s, 16)
                sp.wait_ge(v_biased_s, (j + 1) * TT)
                sp.dma_start(tok_tiles(v_dram, j), v_sb[:, :, :, :].rearrange("p t h w -> p t (h w)")).then_inc(v_out_s, 16)

            def step(i, front, back, more):
                if front:
                    wait(sp, f.y_ready_s, i * TT)
                    sp.dma_start(f.x_res[:, :, :], tok_tiles(x, i)).then_inc(f.res_loaded_s, 16)
                if more:
                    sp.wait_ge(f.ln1.normed_s, (i + 1) * TT)
                    sp.dma_start(f.x_in[:, :, :], tok_tiles(x, i + 1)).then_inc(f.x_loaded_s, 16)
                if back:
                    wait(sp, roped_s, (i - 1) * TT)
                    sp.dma_start(rope_sb[:, :, :, :], rope[bass.ds((i - 1) * CH, CH), :].rearrange(
                        "(t p) (a d) -> p t a d", p=P, a=2)).then_inc(rope_loaded_s, 16)
                    store_back(i - 1)
                if front:
                    sp.wait_ge(f.y_ready_s, (i + 1) * TT)
                    sp.dma_start(tok_tiles(x2_dram, i), f.y[:, :, :]).then_inc(x2_out_s, 16)
            run(sp, step, True)
            sp.wait_ge(x2_out_s, CHUNKS * 16)
            sp.wait_ge(parts_out_s, CHUNKS * PARTS_OUT)
            sp.wait_ge(v_out_s, CHUNKS * 16)

        @block.gpsimd
        def _(pool):
            norm_constants(pool, f, consts_s)
            pool.memset(v_sb[:, :, :, :], 1.0).then_inc(consts_s, 1)
            norm_root(pool, f, f.ln1, 0)

            def rope_tile(j, t):
                n = j * TT + t
                src = qk[:, t % 2, :, :]
                cos = rope_sb[:, t, 0:1, :].to_broadcast([P, HQK, HD])
                sin_low = rope_sb[:, t, 1:2, 0:HD // 2].to_broadcast([P, HQK, HD // 2])
                sin_high = rope_sb[:, t, 1:2, HD // 2:HD].to_broadcast([P, HQK, HD // 2])
                pool.wait_ge(qk_biased_s, n + 1)
                if t == 0:
                    pool.wait_ge(rope_loaded_s, (j + 1) * 16)
                wait(pool, roped_s, n)
                pool.tensor_tensor(qk_cos[:, :, :], src, cos, ALU.mult).then_inc(rope_step_s, 1)
                pool.tensor_tensor(qk_sin[:, :, 0:HD // 2], src[:, :, HD // 2:HD], sin_low, ALU.mult).then_inc(rope_step_s, 1)
                pool.tensor_tensor(qk_sin[:, :, HD // 2:HD], src[:, :, 0:HD // 2], sin_high, ALU.mult).then_inc(rope_step_s, 1)
                pool.wait_ge(rope_step_s, 3 * n + 3)
                wait(pool, roped_t_s, n - 1)
                pool.tensor_tensor(qk_rot[:, t % 2, :], qk_cos[:, :, :].rearrange("p h d -> p (h d)"),
                                   qk_sin[:, :, :].rearrange("p h d -> p (h d)"), ALU.add).then_inc(roped_s, 1)

            def last_part(j, t):
                n = j * TT + t
                pool.wait_ge(part1_s, n + 1)
                if t == 0:
                    wait(pool, parts_out_s, j * PARTS_OUT)
                pool.tensor_tensor(parts[:, 2, :, t * P:(t + 1) * P], rest[:, t % 2, :, :],
                                   parts[:, 1, :, t * P:(t + 1) * P], ALU.subtract).then_inc(part2_s, 1)

            def step(i, front, back, more):
                if more:
                    norm_root(pool, f, f.ln1, i + 1)
                if back:
                    for t in range(TT):
                        rope_tile(i - 1, t)
                        if t:
                            last_part(i - 1, t - 1)
                    last_part(i - 1, TT - 1)
                if front:
                    norm_root(pool, f, ln2, i)
            run(pool, step, True)

        @block.tensor
        def _(pe):
            pe.wait_ge(f.weights_s, WEIGHTS)

            def qkv_tile(j, t):
                n = j * TT + t
                wait(pe, qk_biased_s, n)
                wait(pe, v_biased_s, n)
                for k in range(KD):
                    pe.matmul(qk_bank, x2nT[:, k, t * P:(t + 1) * P], wqkv_sb[:, k, 0:2 * D],
                              start=(k == 0), stop=(k == KD - 1))
                for k in range(KD):
                    last = pe.matmul(v_bank, x2nT[:, k, t * P:(t + 1) * P], wqkv_sb[:, k, 2 * D:3 * D],
                                     start=(k == 0), stop=(k == KD - 1))
                last.then_inc(qkv_s, 1)

            def turn_tile(j, t):
                n = j * TT + t
                pe.wait_ge(roped_s, n + 1)
                wait(pe, rest_s, n - 1)
                for c in range(4):
                    last = pe.transpose(f.tr[t % 2][:, c * P:(c + 1) * P], qk_rot[:, t % 2, c * P:(c + 1) * P], f.ident[:, :])
                last.then_inc(roped_t_s, 1)

            def step(i, front, back, more):
                if front:
                    pe_front(pe, f, i, lambda: wait(pe, rest_s, (i - 1) * TT))
                if back:
                    j = i - 1
                    pe.wait_ge(ln2.normed_s, (j + 1) * TT)
                    if front:
                        pe.wait_ge(f.top_s, (i + 1) * TT)
                    else:
                        pe.wait_ge(rest_s, j * TT)
                    transpose_tokens(pe, f, x2n, f.tr).then_inc(x2_t_s, 1)
                    pe.wait_ge(x2_taken_s, (j + 1) * KD)
                for t in range(TT):
                    if back:
                        qkv_tile(i - 1, t)
                    if front:
                        pe_down(pe, f, i, t)
                    if back and t:
                        turn_tile(i - 1, t - 1)
                if back:
                    turn_tile(i - 1, TT - 1)
            run(pe, step, True)

        @block.scalar
        def _(act):
            act.wait_ge(f.weights_s, WEIGHTS)

            def first_part(j, t):
                n = j * TT + t
                act.wait_ge(roped_t_s, n + 1)
                if t == 0:
                    wait(act, parts_out_s, j * PARTS_OUT)
                act.activation(parts[:, 0, :, t * P:(t + 1) * P],
                               f.tr[t % 2].rearrange("p (c n) -> p c n", n=P), ACT.Copy).then_inc(part0_s, 1)

            def second_part(j, t):
                n = j * TT + t
                act.wait_ge(rest_s, n + 1)
                act.activation(parts[:, 1, :, t * P:(t + 1) * P], rest[:, t % 2, :, :], ACT.Copy).then_inc(part1_s, 1)

            def step(i, front, back, more):
                if front:
                    act_front(act, f, i)
                if back:
                    j = i - 1
                    act.wait_ge(x2_t_s, j + 1)
                    wait(act, qkv_s, j * TT)
                    for k in range(KD):
                        act.activation(x2nT[:, k, :], f.tr[k], ACT.Copy).then_inc(x2_taken_s, 1)
                    for t in range(TT):
                        first_part(j, t)
                        second_part(j, t)
            run(act, step, True)

        @block.vector
        def _(dve):
            def first_norm(i):
                dve.wait_ge(f.x_loaded_s, (i + 1) * 16)
                for t in range(TT):
                    norm_tile_stats(dve, f.ln1, f.x_in, t)
                norm_moments(dve, f.ln1, i)
                wait(dve, f.xn_t_s, i)
                norm_apply(dve, f.ln1, f.x_in, f.xn, i)

            def bias_tile(j, t):
                n = j * TT + t
                dve.wait_ge(qkv_s, n + 1)
                wait(dve, roped_s, n - 1)
                dve.tensor_tensor(qk[:, t % 2, :, :].rearrange("p h d -> p (h d)"), qk_bank,
                                  bqkv_sb[:, 0:2 * D], ALU.add).then_inc(qk_biased_s, 1)
                if t == 0:
                    wait(dve, v_out_s, j * 16)
                dve.tensor_tensor(v_sb[:, t, :, 0:HD], v_bank.rearrange("p (h d) -> p h d", d=HD),
                                  bqkv_sb[:, 2 * D:3 * D].rearrange("p (h d) -> p h d", d=HD),
                                  ALU.add).then_inc(v_biased_s, 1)

            def rest_tile(j, t):
                n = j * TT + t
                dve.wait_ge(part0_s, n + 1)
                wait(dve, part2_s, n - 1)
                dve.tensor_tensor(rest[:, t % 2, :, :], f.tr[t % 2].rearrange("p (c n) -> p c n", n=P),
                                  parts[:, 0, :, t * P:(t + 1) * P], ALU.subtract).then_inc(rest_s, 1)

            dve.wait_ge(f.weights_s, WEIGHTS)
            dve.wait_ge(consts_s, 5)
            first_norm(0)

            def step(i, front, back, more):
                if front:
                    dve_router(dve, f, i)
                if more:
                    first_norm(i + 1)
                if front:
                    dve_gate(dve, f, i)
                    dve.wait_ge(f.res_loaded_s, (i + 1) * 16)
                    wait(dve, x2_out_s, i * 16)
                for t in range(TT):
                    if back:
                        bias_tile(i - 1, t)
                    if front:
                        dve_residual(dve, f, i, t, f.x_res)
                    if back and t:
                        rest_tile(i - 1, t - 1)
                    if front:
                        dve.wait_ge(f.y_ready_s, i * TT + t + 1)
                        norm_tile_stats(dve, ln2, f.y, t)
                if back:
                    rest_tile(i - 1, TT - 1)
                if front:
                    norm_moments(dve, ln2, i)
                    wait(dve, x2_t_s, i)
                    norm_apply(dve, ln2, f.y, x2n, i)
            run(dve, step, True)



def attention_phase(nc, phase, ident, qk_dram, v_dram, ctx_dram):
    def sb(name, shape, dt=F32):
        return phase.enter_context(nc.sbuf_tensor("b_" + name, shape, dt))

    def sem(name):
        return phase.enter_context(nc.semaphore("b_" + name))

    SLOT = QUAD * SEQ
    ident_f = sb("ident_f", [P, P])
    ident_b = sb("ident_b", [P, P], BF16)
    q_stack = sb("q_stack", [STACK, RING * SLOT], BF16)
    k_stack = sb("k_stack", [STACK, RING * SLOT], BF16)
    v_sb = sb("v", [P, KB, QUAD, VW])
    probs = sb("probs", [P, 2, QUAD, CH])
    ctx_sb = sb("ctx_sb", [P, CH])
    PAIRS = QUAD * TT
    KP = SEQ // CH
    UNITS = PAIRS * KP
    maxes = sb("maxes", [P, PAIRS, KP])
    one = sb("one", [P, PAIRS])
    shift = sb("shift", [P, PAIRS])
    shift_rest = sb("shift_rest", [P, 2, PAIRS])
    shift_parts = sb("shift_parts", [P, P], BF16)
    shift_t = sb("shift_t", [PARTS * PAIRS, P], BF16)
    banks = phase.enter_context(nc.psum_tensor("b_banks", [P, 8, CH], F32))
    acc = banks[:, QUAD, :]
    NM = 3
    PASSES = GROUPS * QC
    TURN = 10
    NU = UNITS + 1

    ident_s = sem("ident")
    ones_s = sem("ones")
    one_s = sem("one")
    stack_s = sem("stack")
    v_s = [sem(f"v{p}") for p in range(4)]
    score_s = sem("score_ready")
    exp_s = sem("exped")
    pv_s = sem("pv_done")
    user_s = sem("max_bank_ready")
    freed_s = sem("max_bank_freed")
    shift_s = sem("shift_ready")
    split_s = sem("split_step")
    parts_s = sem("shift_parts")
    rows_s = sem("shift_rows")
    ctx_s = sem("ctx_ready")
    ctx_out_s = sem("ctx_out")
    LOADS = len(Q_PART) * 2 * 16
    ROWS = PARTS * QUAD * 16

    def bank_of(place):
        return banks[:, QUAD + 1 + place % NM, :]

    def done(n, place):
        if isinstance(n, int) and n == 0:
            return place + 1 if place < TURN else place
        if isinstance(n, int) and n == PASSES:
            return n * NU
        return n * NU + place

    def bank_free(n, place):
        first = isinstance(n, int) and n == 0
        before = [p for p in range(place) if p % NM == place % NM and not (first and p == TURN)]
        if isinstance(n, int) and n == PASSES:
            return n * NU - 1
        if before:
            return done(n, before[-1])
        return 0 if first else done(n - 1, max(p for p in range(NU) if p % NM == place % NM))

    def slot_of(n):
        return ((n // QC) % RING) * SLOT

    def run(eng, step):
        step(0, None)
        with eng.Fori(1, QC) as n:
            step(n, None)
        step(QC, 0)
        with eng.Fori(1, PASSES - QC) as m:
            step(m + QC, m)
        step(PASSES, PASSES - QC)
        for m in range(PASSES - QC + 1, PASSES):
            step(None, m)

    with nc.Block() as block:
        @block.sync
        def _(sp):
            sp.dma_start(ident_f[:, :], ident).then_inc(ident_s, 16)

            def load_stacks(g):
                at = (g % RING) * SLOT
                if not (isinstance(g, int) and g < RING):
                    sp.wait_ge(score_s, (g - RING + 1) * QC * KB * 2)
                wait(sp, stack_s, g * LOADS)
                for r in range(len(Q_PART)):
                    for stack, part, which in ((q_stack, Q_PART[r], 0), (k_stack, K_PART[r], 1)):
                        src = qk_dram[bass.ds(g, 1), part, which, :, :].rearrange("g (j d) t -> d (g j) t", d=HD)
                        dst = stack[HD * r:HD * (r + 1), bass.ds(at, SLOT)].rearrange("p (j t) -> p j t", j=QUAD)
                        sp.dma_start(dst, src).then_inc(stack_s, 16)

            def load_v(g, piece):
                rows, cols = SEQ // 4, QUAD * VW
                src = v_dram[bass.ds((g // QC) * SEQ + piece * rows, rows), bass.ds((g % QC) * cols, cols)]
                sp.dma_start(v_sb[:, 4 * piece:4 * piece + 4, :, :].rearrange("p k h w -> p k (h w)"),
                             src.rearrange("(k p) n -> p k n", p=P)).then_inc(v_s[piece], 16)

            def store_rows(n):
                sp.wait_ge(freed_s, done(n + 1, TURN))
                at = slot_of(n) + (n % QC) * CH
                for c in range(PARTS):
                    for j in range(QUAD):
                        first = c * PAIRS + j * TT
                        sp.dma_start(q_stack[SHIFT_ROW + c:SHIFT_ROW + c + 1, bass.ds(at + j * SEQ, CH)],
                                     shift_t[first:first + TT, :]).then_inc(rows_s, 16)

            def store_ctx(m):
                sp.wait_ge(ctx_s, m + 1)
                dst = ctx_dram[bass.ds(m // QC, 1), :, bass.ds((m % QC) * CH, CH)].rearrange("g p t -> (g p) t")
                sp.dma_start(dst, ctx_sb[:, :]).then_inc(ctx_out_s, 16)

            load_stacks(0)
            load_stacks(1)
            for piece in range(4):
                load_v(0, piece)
            for n in range(QC - 1):
                store_rows(n)
            load_stacks(2)

            def chunk(m, g, qc):
                last = isinstance(g, int) and g == GROUPS - 1
                if not last or qc == 0:
                    store_rows(m + QC - 1)
                if not (isinstance(m, int) and m == 0):
                    store_ctx(m - 1)
                if qc == QC - 1 and not last:
                    for piece in range(4):
                        sp.wait_ge(pv_s, m * KB + 4 * piece + 4)
                        load_v(g + 1, piece)

            for qc in range(QC):
                chunk(qc, 0, qc)
            with sp.Fori(1, GROUPS - 2) as g:
                load_stacks(g + 2)
                for qc in range(QC):
                    chunk(g * QC + qc, g, qc)
            for g in (GROUPS - 2, GROUPS - 1):
                for qc in range(QC):
                    chunk(g * QC + qc, g, qc)
            store_ctx(PASSES - 1)
            sp.wait_ge(ctx_out_s, PASSES * 16)

        @block.gpsimd
        def _(pool):
            pool.memset(one[:, :], 1.0).then_inc(one_s, 1)
            pool.wait_ge(one_s, 1)
            pool.memset(k_stack[SR:STACK, :], 1.0).then_inc(ones_s, 1)

            with pool.Fori(0, PASSES) as n:
                pool.wait_ge(shift_s, n + 1)
                pool.tensor_tensor(shift_parts[:, 0 * PAIRS:1 * PAIRS], shift[:, :], one[:, :], ALU.mult).then_inc(split_s, 1)
                pool.wait_ge(split_s, 4 * n + 1)
                pool.tensor_tensor(shift_rest[:, 0, :], shift[:, :], shift_parts[:, 0 * PAIRS:1 * PAIRS], ALU.subtract).then_inc(split_s, 1)
                pool.wait_ge(split_s, 4 * n + 2)
                pool.tensor_tensor(shift_parts[:, 1 * PAIRS:2 * PAIRS], shift_rest[:, 0, :], one[:, :], ALU.mult).then_inc(split_s, 1)
                pool.wait_ge(split_s, 4 * n + 3)
                pool.tensor_tensor(shift_rest[:, 1, :], shift_rest[:, 0, :], shift_parts[:, 1 * PAIRS:2 * PAIRS], ALU.subtract).then_inc(split_s, 1)
                pool.wait_ge(split_s, 4 * n + 4)
                pool.tensor_tensor(shift_parts[:, 2 * PAIRS:3 * PAIRS], shift_rest[:, 1, :], one[:, :], ALU.mult).then_inc(parts_s, 1)

        @block.tensor
        def _(pe):
            pe.wait_ge(ones_s, 3)

            def unit(n, place, slot, at):
                pair, piece = divmod(place - (place > TURN), KP)
                j, tile = divmod(pair, TT)
                wait(pe, freed_s, bank_free(n, place))
                pe.matmul(bank_of(place), q_stack[0:SR, bass.ds(at + (j * SEQ + tile * P), P)],
                          k_stack[0:SR, bass.ds(slot + (j * SEQ + piece * CH), CH)],
                          start=True, stop=True).then_inc(user_s, 1)

            def turn(n):
                pe.wait_ge(parts_s, n)
                pe.wait_ge(freed_s, bank_free(n, TURN))
                pe.transpose(bank_of(TURN)[:, 0:P // 2].bitcast(BF16), shift_parts[:, :], ident_b[:, :]).then_inc(user_s, 1)

            def step(n, m):
                todo = list(range(NU))
                if n is None or (isinstance(n, int) and n == PASSES):
                    todo = [] if n is None else [TURN]
                elif isinstance(n, int) and n == 0:
                    todo.remove(TURN)
                if len(todo) > 1:
                    pe.wait_ge(stack_s, (n // QC + 1) * LOADS)
                    slot = pe.snap(slot_of(n)) if not isinstance(n, int) else slot_of(n)
                    at = pe.snap(slot + (n % QC) * CH) if not isinstance(n, int) else slot + (n % QC) * CH

                def users(count):
                    for _ in range(min(count, len(todo))):
                        place = todo.pop(0)
                        if place == TURN:
                            turn(n)
                        else:
                            unit(n, place, slot, at)

                if m is None:
                    users(NU)
                    return
                pe.wait_ge(rows_s, (m + QC - 1) * ROWS if not isinstance(m, int) else min(m + QC - 1, PASSES) * ROWS)
                kslot = pe.snap(slot_of(m)) if not isinstance(m, int) else slot_of(m)
                qat = pe.snap(kslot + (m % QC) * CH) if not isinstance(m, int) else kslot + (m % QC) * CH

                def scores(kb, half):
                    for j in (2 * half, 2 * half + 1):
                        last = pe.matmul(banks[:, j, :], k_stack[:, bass.ds(kslot + (j * SEQ + kb * P), P)],
                                         q_stack[:, bass.ds(qat + j * SEQ, CH)], start=True, stop=True)
                    last.then_inc(score_s, 1)

                def add_values(kb):
                    if kb == 0:
                        wait(pe, ctx_s, m)
                    if kb % 4 == 0:
                        pe.wait_ge(v_s[kb // 4], (m // QC + 1) * 16)
                    for j in range(QUAD):
                        last = pe.matmul(acc[VW * j:VW * (j + 1), :], v_sb[:, kb, j, :], probs[:, kb % 2, j, :],
                                         start=(kb == 0), stop=(kb == KB - 1))
                    last.then_inc(pv_s, 1)

                for kb in range(KB):
                    s = m * KB + kb
                    wait(pe, exp_s, 2 * s - 1)
                    scores(kb, 0)
                    users(1)
                    wait(pe, exp_s, 2 * s)
                    scores(kb, 1)
                    users(1)
                    if kb:
                        add_values(kb - 1)
                        users(2)
                users(NU)
                pe.wait_ge(exp_s, 2 * (m + 1) * KB)
                add_values(KB - 1)
            run(pe, step)

        @block.scalar
        def _(act):
            act.wait_ge(ident_s, 16)
            act.activation(ident_b[:, :], ident_f[:, :], ACT.Copy).then_inc(ones_s, 1)
            act.activation(shift_parts[:, PARTS * PAIRS:P], ident_f[:, PARTS * PAIRS:P], ACT.Copy, scale=0.0).then_inc(ones_s, 1)

            def step(n, m):
                if m is None:
                    return
                for kb in range(KB):
                    s = m * KB + kb
                    for half in range(2):
                        act.wait_ge(score_s, 2 * s + half + 1)
                        if half == 0:
                            wait(act, pv_s, s - 1)
                        act.activation(probs[:, kb % 2, 2 * half:2 * half + 2, :], banks[:, 2 * half:2 * half + 2, :],
                                       ACT.Exp, scale=SCORE_SCALE).then_inc(exp_s, 1)
                act.wait_ge(pv_s, (m + 1) * KB)
                wait(act, ctx_out_s, m * 16)
                act.activation(ctx_sb[:, :], acc, ACT.Copy).then_inc(ctx_s, 1)
            step(None, 0)
            with act.Fori(1, PASSES) as m:
                step(None, m)

        @block.vector
        def _(dve):
            def turned(n):
                dve.wait_ge(user_s, done(n, TURN))
                wait(dve, rows_s, (n - 1) * ROWS)
                dve.tensor_copy(shift_t[:, :], bank_of(TURN)[0:PARTS * PAIRS, 0:P // 2].bitcast(BF16)).then_inc(freed_s, 1)

            def pass_max(n):
                wait(dve, shift_s, n)
                for place in range(NU):
                    if place == TURN:
                        if not (isinstance(n, int) and n == 0):
                            turned(n)
                        continue
                    pair, piece = divmod(place - (place > TURN), KP)
                    dve.wait_ge(user_s, done(n, place))
                    dve.reduce_max(maxes[:, pair, piece:piece + 1], bank_of(place), axis=X).then_inc(freed_s, 1)
                dve.wait_ge(freed_s, done(n, NU - 1))
                wait(dve, parts_s, n)
                dve.tensor_reduce(shift[:, :], maxes[:, :, :], X, ALU.max, negate=True).then_inc(shift_s, 1)
            pass_max(0)
            pass_max(1)
            with dve.Fori(2, PASSES) as n:
                pass_max(n)
            turned(PASSES)



def output_phase(nc, phase, wo, bo, router, w1, b1, w2, b2, ident, x2_dram, ctx_dram, out):
    def sb(name, shape, dt=F32):
        return phase.enter_context(nc.sbuf_tensor("c_" + name, shape, dt))

    def sem(name):
        return phase.enter_context(nc.semaphore("c_" + name))

    f = ffn_buffers(nc, phase, "c_")
    wo_sb = sb("wo", [P, KD, D])
    bo_sb = sb("bo", [P, D])
    x2_sb = sb("x2", [P, TT, D])
    raw = sb("raw", [P, QUAD, CH])
    sum_rec = sb("sum_rec", [P, 2, HEADS])
    context = sb("context", [P, TT, D])
    contextT = sb("contextT", [P, KD, CH])
    projected = sb("projected", [P, TT, D])
    proj_banks = [f.banks[:, 6 + k, 0:D] for k in range(2)]

    consts_s = sem("consts")
    raw_loaded_s = sem("raw_loaded")
    x2_loaded_s = sem("x2_loaded")
    raw_t_s = sem("raw_t")
    sum_rec_s = sem("sum_rec")
    context_s = sem("context_ready")
    context_t_s = sem("context_t")
    context_taken_s = sem("context_taken")
    proj_s = sem("proj")
    proj_bias_s = sem("proj_bias")
    x3_s = sem("x3")
    out_s = sem("out")
    WEIGHTS = FFN_WEIGHTS + 2 * 16

    def run(eng, step):
        step(-1, front=False, more=True)
        step(0, front=True, more=True)
        with eng.Fori(1, CHUNKS - 1) as i:
            step(i, front=True, more=True)
        step(CHUNKS - 1, front=True, more=False)

    with nc.Block() as block:
        @block.sync
        def _(sp):
            def load_pre(j):
                batch, at = j // QC, (j % QC) * CH
                wait(sp, raw_t_s, j * TT)
                sp.dma_start(raw[:, :, :], ctx_dram[bass.ds(batch * 4, 4), :, bass.ds(at, CH)].rearrange(
                    "g p t -> p g t")).then_inc(raw_loaded_s, 16)
                wait(sp, x3_s, j * TT)
                sp.dma_start(x2_sb[:, :, :], tok_tiles(x2_dram, j)).then_inc(x2_loaded_s, 16)

            def step(i, front, more):
                if more:
                    load_pre(i + 1)
                if front:
                    sp.wait_ge(f.y_ready_s, (i + 1) * TT)
                    sp.dma_start(tok_tiles(out, i), f.y[:, :, :]).then_inc(out_s, 16)
            load_ffn_weights(sp, f, router, w1, b1, w2, b2, ident)
            sp.dma_start(wo_sb[:, :, :], wo.rearrange("(k p) n -> p k n", p=P)).then_inc(f.weights_s, 16)
            sp.dma_start(bo_sb[:, :], bo.partition_broadcast(P)).then_inc(f.weights_s, 16)
            run(sp, step)
            sp.wait_ge(out_s, CHUNKS * 16)

        @block.gpsimd
        def _(pool):
            norm_constants(pool, f, consts_s)

            def step(i, front, more):
                if more:
                    norm_root(pool, f, f.ln1, i + 1)
                    wait(pool, f.y_ready_s, (i + 1) * TT)
                    pool.wait_ge(x3_s, (i + 2) * TT)
                    pool.tensor_tensor(f.x_res[:, :, :], f.x_in[:, :, :],
                                       f.consts[:, 3, :].unsqueeze(2).to_broadcast([P, TT, D]), ALU.mult).then_inc(f.res_copied_s, 1)
            run(pool, step)

        @block.tensor
        def _(pe):
            pe.wait_ge(f.weights_s, WEIGHTS)

            def pre(j, first):
                pe.wait_ge(raw_loaded_s, (j + 1) * 16)
                for t in range(TT):
                    wait(pe, context_s, j * TT + t - 1)
                    if t < 2 and not first:
                        pe.wait_ge(f.top_s, j * TT)
                    for g in range(QUAD):
                        last = pe.transpose(f.tr[t % 2][:, g * P:(g + 1) * P], raw[:, g, t * P:(t + 1) * P], f.ident[:, :])
                    last.then_inc(raw_t_s, 1)
                pe.wait_ge(context_s, (j + 1) * TT)
                transpose_tokens(pe, f, context, f.tr).then_inc(context_t_s, 1)
                pe.wait_ge(context_taken_s, (j + 1) * KD)
                for t in range(TT):
                    wait(pe, proj_bias_s, j * TT + t - 1)
                    for k in range(KD):
                        last = pe.matmul(proj_banks[t % 2], contextT[:, k, t * P:(t + 1) * P], wo_sb[:, k, :],
                                         start=(k == 0), stop=(k == KD - 1))
                    last.then_inc(proj_s, 1)

            def step(i, front, more):
                if front:
                    pe_front(pe, f, i, lambda: pe.wait_ge(context_taken_s, (i + 1) * KD))
                if more:
                    pre(i + 1, not front)
                if front:
                    for t in range(TT):
                        pe_down(pe, f, i, t)
            run(pe, step)

        @block.scalar
        def _(act):
            act.wait_ge(f.weights_s, WEIGHTS)

            def step(i, front, more):
                if front:
                    act_front(act, f, i)
                if more:
                    j = i + 1
                    act.wait_ge(context_t_s, j + 1)
                    wait(act, proj_s, j * TT)
                    for k in range(KD):
                        act.activation(contextT[:, k, :], f.tr[k], ACT.Copy).then_inc(context_taken_s, 1)
            run(act, step)

        @block.vector
        def _(dve):
            dve.wait_ge(f.weights_s, WEIGHTS)

            def divide(j, t):
                n = j * TT + t
                raw_t = f.tr[t % 2].rearrange("p (h w) -> p h w", w=VW)
                dve.wait_ge(raw_t_s, n + 1)
                if t == 0:
                    wait(dve, context_t_s, j)
                dve.reciprocal(sum_rec[:, t % 2, :].unsqueeze(2), raw_t[:, :, HD:HD + 1]).then_inc(sum_rec_s, 1)
                dve.wait_ge(sum_rec_s, n + 1)
                dve.tensor_tensor(context[:, t, :].rearrange("p (h d) -> p h d", d=HD), raw_t[:, :, 0:HD],
                                  sum_rec[:, t % 2, :].unsqueeze(2).to_broadcast([P, HEADS, HD]), ALU.mult).then_inc(context_s, 1)

            def add_output(j, t):
                n = j * TT + t
                dve.wait_ge(proj_s, n + 1)
                if t == 0:
                    dve.wait_ge(x2_loaded_s, (j + 1) * 16)
                    wait(dve, f.res_copied_s, j)
                dve.tensor_tensor(projected[:, t, :], proj_banks[t % 2], bo_sb[:, :], ALU.add).then_inc(proj_bias_s, 1)
                dve.wait_ge(proj_bias_s, n + 1)
                dve.tensor_tensor(f.x_in[:, t, :], projected[:, t, :], x2_sb[:, t, :], ALU.add).then_inc(x3_s, 1)

            def step(i, front, more):
                if front:
                    dve_router(dve, f, i)
                if more:
                    j = i + 1
                    for t in range(TT):
                        divide(j, t)
                if front:
                    dve_gate(dve, f, i)
                if more:
                    for t in range(TT):
                        add_output(j, t)
                        dve.wait_ge(x3_s, j * TT + t + 1)
                        norm_tile_stats(dve, f.ln1, f.x_in, t)
                    norm_moments(dve, f.ln1, j)
                    wait(dve, f.xn_t_s, j)
                    norm_apply(dve, f.ln1, f.x_in, f.xn, j)
                if front:
                    dve.wait_ge(f.res_copied_s, i + 1)
                    wait(dve, out_s, i * 16)
                    for t in range(TT):
                        dve_residual(dve, f, i, t, f.x_res)
            run(dve, step)


def rope_table():
    import numpy as np

    half = HD // 2
    inv = (np.float32(1.0) / np.power(np.float32(10000.0), np.arange(half, dtype=np.float32) / np.float32(half))).astype(np.float32)
    angle = np.outer(np.arange(SEQ, dtype=np.float32), inv).astype(np.float32)
    cos, sin = np.cos(angle), np.sin(angle)
    table = np.concatenate([cos, cos, -sin, sin], axis=1).astype(np.float32)
    return np.tile(table, (BATCH, 1))


def kernel(**inputs):
    import numpy as np
    from concourse import bacc
    from concourse.bass_utils import run_bass_kernel_spmd

    a = {name: np.asarray(value) for name, value in inputs.items()}
    arrays = {
        "x": a["L0_attn_x"].reshape(TOKENS, D),
        "wqkv": np.concatenate([a["L0_attn_Wq"].T, a["L0_attn_Wk"].T, a["L0_attn_Wv"].T], axis=1),
        "bqkv": np.concatenate([a["L0_attn_bq"], a["L0_attn_bk"], a["L0_attn_bv"]]).reshape(1, 3 * D),
        "wo": a["L0_attn_Wo"].T,
        "bo": a["L0_attn_bo"].reshape(1, D),
        "router": a["L0_ffn_router_w"],
        "w1": a["L0_ffn_w1"],
        "b1": a["L0_ffn_b1"].reshape(FB, P).T,
        "w2": a["L0_ffn_w2"],
        "b2": a["L0_ffn_b2"].reshape(1, D),
        "rope": rope_table(),
        "ident": np.eye(P, dtype=np.float32),
    }
    arrays = {name: np.ascontiguousarray(value) for name, value in arrays.items()}
    nc = bacc.Bacc("TRN2", target_bir_lowering=False, num_devices=1)
    ins = [nc.dram_tensor(name, v.shape, mybir.dt.from_np(v.dtype), kind="ExternalInput").ap() for name, v in arrays.items()]
    out = nc.dram_tensor("out", (TOKENS, D), F32, kind="ExternalOutput").ap()
    build(nc, *ins, out)
    got = run_bass_kernel_spmd(nc, [arrays], core_ids=[0])
    return got.results[0]["out"].reshape(BATCH, SEQ, D)
```

```python
from contextlib import ExitStack

import concourse.bass as bass
from concourse import mybir

ALU = mybir.AluOpType
ACT = mybir.ActivationFunctionType
F32 = mybir.dt.float32
BF16 = mybir.dt.bfloat16
F32R = mybir.dt.float32r
X = mybir.AxisListType.X

P = 128
BATCH, SEQ, D = 4, 2048, 256
HEADS, HD = 16, 16
FF, EXPERTS, TOP_K = 1024, 8, 2
TOKENS = BATCH * SEQ
EPS = 1e-5

KD = D // P
FB = FF // P
CH = 512
TT = CH // P
CHUNKS = TOKENS // CH

QUAD = 4
GROUPS = BATCH * HEADS // QUAD
QC = SEQ // CH
KB = SEQ // P
VW = 32
PARTS = 3
Q_PART = (0, 0, 0, 1, 1, 2)
K_PART = (0, 1, 2, 0, 1, 0)
SR = HD * len(Q_PART)
SHIFT_ROW = SR
STACK = SR + PARTS
RING = 3
SCORE_SCALE = HD ** -0.5


def wait(eng, sem, value):
    if not (isinstance(value, int) and value <= 0):
        eng.wait_ge(sem, value)


def build(nc, x, wqkv, bqkv, wo, bo, router, w1, b1, w2, b2, rope, ident, out):
    ctx = ExitStack()
    with ctx:
        x2_dram = nc.dram_tensor("x2_dram", (TOKENS, D), F32, kind="Internal").ap()
        qk_dram = nc.dram_tensor("qk_dram", (BATCH, PARTS * 2 * D, SEQ), BF16, kind="Internal").ap()
        v_dram = nc.dram_tensor("v_dram", (TOKENS, HEADS * VW), F32, kind="Internal").ap()
        ctx_dram = nc.dram_tensor("ctx_dram", (GROUPS, P, SEQ), F32, kind="Internal").ap()
        with ExitStack() as phase:
            project_phase(nc, phase, x, wqkv, bqkv, router, w1, b1, w2, b2, rope, ident, x2_dram, qk_dram, v_dram)
        with ExitStack() as phase:
            attention_phase(nc, phase, ident, qk_dram, v_dram, ctx_dram)
        with ExitStack() as phase:
            output_phase(nc, phase, wo, bo, router, w1, b1, w2, b2, ident, x2_dram, ctx_dram, out)


def tok_tiles(ap, chunk):
    return ap[bass.ds(chunk * CH, CH), :].rearrange("(t p) n -> p t n", p=P)



class Buffers:
    pass


def allocators(nc, phase, pre):
    def sb(name, shape, dt=F32):
        return phase.enter_context(nc.sbuf_tensor(pre + name, shape, dt))

    def sem(name):
        return phase.enter_context(nc.semaphore(pre + name))
    return sb, sem


def split_pair(sb, name, shape):
    return sb(name + "_hi", shape, F32R), sb(name + "_lo", shape, F32R)


def ffn_buffers(nc, phase, pre):
    sb, sem = allocators(nc, phase, pre)
    f = Buffers()
    f.w1_raw = sb("w1_raw", [P, KD, FF])
    f.w2_raw = sb("w2_raw", [P, FB, D])
    f.router_raw = sb("router_raw", [P, KD, EXPERTS])
    f.w1 = split_pair(sb, "w1", [P, KD, FF])
    f.w2 = split_pair(sb, "w2", [P, FB, D])
    f.router = split_pair(sb, "router", [P, KD, P])
    f.b1 = sb("b1", [P, FB])
    f.b2 = sb("b2", [P, D])
    f.ident = sb("ident", [P, P])
    f.consts = sb("consts", [P, 4, TT])
    f.x_in = sb("x_in", [P, TT, D])
    f.x_res = sb("x_res", [P, TT, D])
    f.xn = sb("xn", [P, TT, D])
    f.xnT = split_pair(sb, "xnT", [P, KD, CH])
    f.hidden = sb("hidden", [P, 2, CH])
    f.hT = split_pair(sb, "hT", [P, FB, CH])
    f.logitsT = sb("logitsT", [P, CH])
    f.ffn_out = sb("ffn_out", [P, TT, D])
    f.y = sb("y", [P, TT, D])
    f.top = sb("top", [P, TT, EXPERTS])
    f.top_max = sb("top_max", [P, TT])
    f.top_shift = sb("top_shift", [P, TT, EXPERTS])
    f.top_exp = sb("top_exp", [P, TT, EXPERTS])
    f.exp_sum = sb("exp_sum", [P, TT])
    f.exp_rec = sb("exp_rec", [P, TT])
    f.top_prob = sb("top_prob", [P, TT, TOP_K])
    f.top_sum = sb("top_sum", [P, TT])
    f.top_rec = sb("top_rec", [P, TT])
    f.combine = sb("combine", [P, TT, TOP_K])
    f.gate = sb("gate", [P, TT])
    f.gate_half = sb("gate_half", [P, TT])
    f.banks = phase.enter_context(nc.psum_tensor(pre + "banks", [P, 8, CH], F32))
    f.tr = [f.banks[:, k, :] for k in range(2)]
    f.up = [f.banks[:, 2 + k, :] for k in range(2)]
    f.down = [f.banks[:, 4 + k, 0:D] for k in range(2)]
    f.logits = f.up[1].rearrange("p (t e) -> p t e", e=P)[:, :, 0:EXPERTS]
    f.weights_s = sem("weights")
    f.split_hi_s = sem("split_hi")
    f.split_lo_s = sem("split_lo")
    f.x_loaded_s = sem("x_loaded")
    f.res_loaded_s = sem("res_loaded")
    f.res_copied_s = sem("res_copied")
    f.xn_t_s = sem("xn_t")
    f.xn_hi_s = sem("xn_hi")
    f.xn_lo_s = sem("xn_lo")
    f.up_s = sem("up")
    f.h_hi_s = sem("h_hi")
    f.h_s = sem("h")
    f.h_lo_s = sem("h_lo")
    f.down_s = sem("down")
    f.logits_t_s = sem("logits_t")
    f.logits_taken_s = sem("logits_taken")
    f.logits_s = sem("logits")
    f.top_max_s = sem("top_max")
    f.top_s = sem("top")
    f.shifted_s = sem("shifted")
    f.exped_s = sem("exped")
    f.gate_step_s = sem("gate_step")
    f.half_s = sem("half")
    f.ffn_sum_s = sem("ffn_sum")
    f.y_ready_s = sem("y_ready")
    f.ln1 = norm_buffers(nc, phase, pre + "ln1_")
    return f


def norm_buffers(nc, phase, pre):
    sb, sem = allocators(nc, phase, pre)
    n = Buffers()
    n.stats = sb("stats", [P, TT, 6])
    n.moments = sb("moments", [P, TT, 2])
    n.fence = sb("fence", [P, 1])
    n.var = sb("var", [P, TT])
    n.guess = sb("guess", [P, TT])
    n.square = sb("square", [P, TT])
    n.product = sb("product", [P, TT])
    n.half = sb("half", [P, TT])
    n.factor = sb("factor", [P, TT])
    n.rstd = sb("rstd", [P, TT])
    n.stats_s = sem("stats_s")
    n.moments_s = sem("moments_s")
    n.root_step_s = sem("root_step_s")
    n.rstd_s = sem("rstd_s")
    n.normed_s = sem("normed_s")
    return n


FFN_WEIGHTS = 6 * 16


def load_ffn_weights(sp, f, router, w1, b1, w2, b2, ident):
    sp.dma_start(f.ident[:, :], ident).then_inc(f.weights_s, 16)
    sp.dma_start(f.router_raw[:, :, :], router.rearrange("(k p) e -> p k e", p=P)).then_inc(f.weights_s, 16)
    sp.dma_start(f.w1_raw[:, :, :], w1.rearrange("(k p) n -> p k n", p=P)).then_inc(f.weights_s, 16)
    sp.dma_start(f.b1[:, :], b1).then_inc(f.weights_s, 16)
    sp.dma_start(f.w2_raw[:, :, :], w2.rearrange("(k p) n -> p k n", p=P)).then_inc(f.weights_s, 16)
    sp.dma_start(f.b2[:, :], b2.partition_broadcast(P)).then_inc(f.weights_s, 16)


def flat(ap):
    return ap.rearrange("p k n -> p (k n)")


def act_split_weights(act, f, pairs):
    for part in f.router:
        act.activation(part[:, :, EXPERTS:P], f.w1_raw[:, :, EXPERTS:P], ACT.Copy, scale=0.0).then_inc(f.split_hi_s, 1)
    for raw, (hi, lo), cols in pairs:
        act.activation(hi[:, :, 0:cols], raw[:, :, :], ACT.Copy).then_inc(f.split_hi_s, 1)


def dve_split_weights(dve, f, pairs):
    for k, (raw, (hi, lo), cols) in enumerate(pairs):
        dve.wait_ge(f.split_hi_s, 3 + k)
        dve.tensor_tensor(lo[:, :, 0:cols], raw[:, :, :], hi[:, :, 0:cols].bitcast(F32), ALU.subtract).then_inc(f.split_lo_s, 1)


def ffn_pairs(f):
    return [(f.router_raw, f.router, EXPERTS), (f.w1_raw, f.w1, FF), (f.w2_raw, f.w2, D)]


def product(pe, out, left, right, blocks):
    n = 0
    for k in range(blocks):
        for a, b in ((0, 0), (0, 1), (1, 0)):
            last = pe.matmul(out, left(a, k), right(b, k), start=(n == 0), stop=(n == 3 * blocks - 1))
            n += 1
    return last


def norm_stats(dve, n, src, t):
    dve.bn_stats(n.stats[:, t, :], src[:, t, :]).then_inc(n.stats_s, 1)


def norm_moments(dve, n, i):
    dve.wait_ge(n.stats_s, (i + 1) * TT)
    dve.tensor_copy(n.fence[:, :], n.stats[:, TT - 1, 0:1])
    for t in range(TT):
        dve.bn_aggr(n.moments[:, t, :], n.stats[:, t, :]).then_inc(n.moments_s, 1)


def norm_apply(dve, n, src, dst, i, t):
    dve.wait_ge(n.rstd_s, i + 1)
    dve.tensor_scalar(dst[:, t, :], src[:, t, :], n.moments[:, t, 0:1], n.rstd[:, t:t + 1],
                      ALU.subtract, ALU.mult).then_inc(n.normed_s, 1)


ROOT_STEPS = 6


def norm_constants(pool, f, consts_s):
    for k, value in enumerate((EPS, -0.5, 1.5, 1.0)):
        pool.memset(f.consts[:, k, :], value).then_inc(consts_s, 1)
    pool.wait_ge(consts_s, 4)


def norm_root(pool, f, n, i):
    eps, minus_half, three_halves = (f.consts[:, k, :] for k in range(3))
    steps = (
        (n.var, n.moments[:, :, 1], eps, ALU.add),
        (n.guess, n.var[:, :], minus_half, ALU.pow),
        (n.square, n.guess[:, :], n.guess[:, :], ALU.mult),
        (n.product, n.square[:, :], n.var[:, :], ALU.mult),
        (n.half, n.product[:, :], minus_half, ALU.mult),
        (n.factor, n.half[:, :], three_halves, ALU.add),
    )
    pool.wait_ge(n.moments_s, i * TT + TT)
    wait(pool, n.normed_s, i * TT)
    for k, (dst, in0, in1, op) in enumerate(steps):
        if k:
            pool.wait_ge(n.root_step_s, i * ROOT_STEPS + k)
        pool.tensor_tensor(dst[:, :], in0, in1, op).then_inc(n.root_step_s, 1)
    pool.wait_ge(n.root_step_s, i * ROOT_STEPS + ROOT_STEPS)
    pool.tensor_tensor(n.rstd[:, :], n.guess[:, :], n.factor[:, :], ALU.mult).then_inc(n.rstd_s, 1)


def transpose_tokens(pe, f, src):
    for k in range(KD):
        for t in range(TT):
            last = pe.transpose(f.tr[k][:, t * P:(t + 1) * P], src[:, t, k * P:(k + 1) * P], f.ident[:, :])
    return last


def take_hi(act, f, dst, k, sem):
    act.activation(dst[0][:, k, :], f.tr[k], ACT.Copy).then_inc(sem, 1)


def take_lo(dve, f, dst, k, i, hi_s, lo_s):
    dve.wait_ge(hi_s, i * KD + k + 1)
    dve.tensor_tensor(dst[1][:, k, :], f.tr[k], dst[0][:, k, :].bitcast(F32), ALU.subtract).then_inc(lo_s, 1)


def pe_up(pe, f, i, b):
    if b == 0:
        pe.wait_ge(f.xn_hi_s, (i + 1) * KD)
        pe.wait_ge(f.xn_lo_s, (i + 1) * KD)
    if b == 1:
        pe.wait_ge(f.top_s, (i + 1) * TT)
    wait(pe, f.h_s, i * FB + b - 1)
    product(pe, f.up[b % 2], lambda c, k: f.w1[c][:, k, b * P:(b + 1) * P],
            lambda c, k: f.xnT[c][:, k, :], KD).then_inc(f.up_s, 1)


def pe_logits(pe, f, i):
    pe.wait_ge(f.xn_hi_s, (i + 1) * KD)
    pe.wait_ge(f.xn_lo_s, (i + 1) * KD)
    wait(pe, f.h_s, i * FB)
    product(pe, f.up[0], lambda c, k: f.router[c][:, k, :], lambda c, k: f.xnT[c][:, k, :], KD).then_inc(f.logits_t_s, 1)


def pe_turn_logits(pe, f, i):
    pe.wait_ge(f.logits_taken_s, i + 1)
    for t in range(TT):
        last = pe.transpose(f.up[1][:, t * P:(t + 1) * P], f.logitsT[:, t * P:(t + 1) * P], f.ident[:, :])
    last.then_inc(f.logits_s, 1)


def pe_down(pe, f, i, t):
    if t == 0:
        pe.wait_ge(f.h_hi_s, (i + 1) * FB)
        pe.wait_ge(f.h_lo_s, (i + 1) * FB)
    wait(pe, f.ffn_sum_s, i * TT + t - 1)
    product(pe, f.down[t % 2], lambda c, k: f.hT[c][:, k, t * P:(t + 1) * P],
            lambda c, k: f.w2[c][:, k, :], FB).then_inc(f.down_s, 1)


def act_gelu(act, f, i, b):
    act.wait_ge(f.up_s, i * FB + b + 1)
    if b == 0:
        wait(act, f.down_s, i * TT)
    act.activation(f.hT[0][:, b, :], f.up[b % 2], ACT.Gelu_apprx_tanh, bias=f.b1[:, b:b + 1]).then_inc(f.h_hi_s, 1)
    wait(act, f.h_lo_s, i * FB + b - 1)
    act.activation(f.hidden[:, b % 2, :], f.up[b % 2], ACT.Gelu_apprx_tanh, bias=f.b1[:, b:b + 1]).then_inc(f.h_s, 1)


def dve_gelu_lo(dve, f, i, b):
    dve.wait_ge(f.h_s, i * FB + b + 1)
    if b == 0:
        wait(dve, f.down_s, i * TT)
    dve.tensor_tensor(f.hT[1][:, b, :], f.hidden[:, b % 2, :], f.hT[0][:, b, :].bitcast(F32),
                      ALU.subtract).then_inc(f.h_lo_s, 1)


def act_take_logits(act, f, i):
    act.wait_ge(f.logits_t_s, i + 1)
    wait(act, f.logits_s, i)
    act.activation(f.logitsT[:, :], f.up[0], ACT.Copy).then_inc(f.logits_taken_s, 1)


def act_router_exp(act, f, i):
    act.wait_ge(f.shifted_s, i + 1)
    wait(act, f.gate_step_s, i * GATE_STEPS)
    act.activation(f.top_exp[:, :, :], f.top_shift[:, :, :], ACT.Exp).then_inc(f.exped_s, 1)


def dve_router(dve, f, i):
    dve.wait_ge(f.logits_s, i + 1)
    dve.reduce_max(f.top_max[:, :], f.logits, axis=X).then_inc(f.top_max_s, 1)
    for t in range(TT):
        dve.max(f.top[:, t, :], f.logits[:, t, :]).then_inc(f.top_s, 1)
    dve.wait_ge(f.top_max_s, i + 1)
    dve.wait_ge(f.top_s, (i + 1) * TT)
    wait(dve, f.exped_s, i)
    dve.tensor_tensor(f.top_shift[:, :, :], f.top[:, :, :], f.top_max[:, :].unsqueeze(2).to_broadcast([P, TT, EXPERTS]),
                      ALU.subtract).then_inc(f.shifted_s, 1)


GATE_STEPS = 7


def dve_gate(dve, f, i):
    s, base = f.gate_step_s, i * GATE_STEPS
    dve.wait_ge(f.exped_s, i + 1)
    dve.reduce_sum(f.exp_sum[:, :], f.top_exp[:, :, :], axis=X).then_inc(s, 1)
    dve.wait_ge(s, base + 1)
    dve.reciprocal(f.exp_rec[:, :], f.exp_sum[:, :]).then_inc(s, 1)
    dve.wait_ge(s, base + 2)
    dve.tensor_tensor(f.top_prob[:, :, :], f.top_exp[:, :, 0:TOP_K],
                      f.exp_rec[:, :].unsqueeze(2).to_broadcast([P, TT, TOP_K]), ALU.mult).then_inc(s, 1)
    dve.wait_ge(s, base + 3)
    dve.reduce_sum(f.top_sum[:, :], f.top_prob[:, :, :], axis=X).then_inc(s, 1)
    dve.wait_ge(s, base + 4)
    dve.reciprocal(f.top_rec[:, :], f.top_sum[:, :]).then_inc(s, 1)
    dve.wait_ge(s, base + 5)
    dve.tensor_tensor(f.combine[:, :, :], f.top_prob[:, :, :],
                      f.top_rec[:, :].unsqueeze(2).to_broadcast([P, TT, TOP_K]), ALU.mult).then_inc(s, 1)
    dve.wait_ge(s, base + 6)
    dve.reduce_sum(f.gate[:, :], f.combine[:, :, :], axis=X).then_inc(s, 1)
    dve.wait_ge(s, base + 7)
    dve.tensor_scalar(f.gate_half[:, :], f.gate[:, :], 0.5, None, ALU.mult).then_inc(f.half_s, 1)


def dve_residual(dve, f, i, t, res):
    dve.wait_ge(f.down_s, i * TT + t + 1)
    dve.tensor_tensor(f.ffn_out[:, t, :], f.down[t % 2], f.b2[:, :], ALU.add).then_inc(f.ffn_sum_s, 1)
    if t == 0:
        dve.wait_ge(f.half_s, i + 1)
    dve.wait_ge(f.ffn_sum_s, i * TT + t + 1)
    dve.scalar_tensor_tensor(f.y[:, t, :], f.ffn_out[:, t, :], f.gate_half[:, t:t + 1], res[:, t, :],
                             ALU.mult, ALU.add).then_inc(f.y_ready_s, 1)



def project_phase(nc, phase, x, wqkv, bqkv, router, w1, b1, w2, b2, rope, ident, x2_dram, qk_dram, v_dram):
    sb, sem = allocators(nc, phase, "a_")
    f = ffn_buffers(nc, phase, "a_")
    ln2 = norm_buffers(nc, phase, "a_ln2_")
    HQK = 2 * HEADS
    wqkv_raw = sb("wqkv_raw", [P, KD, 3 * D])
    wqkv_sb = split_pair(sb, "wqkv", [P, KD, 3 * D])
    bqkv_sb = sb("bqkv", [P, 3 * D])
    x2n = sb("x2n", [P, TT, D])
    x2nT = split_pair(sb, "x2nT", [P, KD, CH])
    rope_sb = sb("rope_sb", [P, TT, 2, HD])
    qk = sb("qk", [P, 2, HQK, HD])
    qk_cos = sb("qk_cos", [P, HQK, HD])
    qk_sin = sb("qk_sin", [P, HQK, HD])
    qk_rot = sb("qk_rot", [P, 2, HQK * HD])
    rest = sb("rest", [P, 2, 4, P])
    parts = sb("parts", [P, PARTS, 4, CH], BF16)
    v_sb = sb("v_sb", [P, TT, HEADS, VW])
    qk_bank = f.banks[:, 6, :]
    v_bank = f.banks[:, 7, 0:D]

    consts_s = sem("consts")
    rope_loaded_s = sem("rope_loaded")
    x2_t_s = sem("x2_t")
    x2_hi_s = sem("x2_hi")
    x2_lo_s = sem("x2_lo")
    qkv_s = sem("qkv")
    qk_biased_s = sem("qk_biased")
    v_biased_s = sem("v_biased")
    rope_step_s = sem("rope_step")
    roped_s = sem("roped")
    roped_t_s = sem("roped_t")
    part0_s = sem("part0")
    rest_s = sem("rest_ready")
    part1_s = sem("part1")
    part2_s = sem("part2")
    x2_out_s = sem("x2_out")
    parts_out_s = sem("parts_out")
    v_out_s = sem("v_out")
    WEIGHTS = FFN_WEIGHTS + 2 * 16
    pairs = ffn_pairs(f) + [(wqkv_raw, wqkv_sb, 3 * D)]

    def run(eng, step):
        step(-1, ahead=True, load=True)
        step(0, front=True, ahead=True, load=True)
        step(1, front=True, back=True, ahead=True, load=True)
        with eng.Fori(2, CHUNKS - 2) as i:
            step(i, front=True, back=True, late=True, ahead=True, load=True)
        step(CHUNKS - 2, front=True, back=True, late=True, ahead=True)
        step(CHUNKS - 1, front=True, back=True, late=True)
        step(CHUNKS, back=True, late=True)
        step(CHUNKS + 1, late=True)

    with nc.Block() as block:
        @block.sync
        def _(sp):
            load_ffn_weights(sp, f, router, w1, b1, w2, b2, ident)
            sp.dma_start(wqkv_raw[:, :, :], wqkv.rearrange("(k p) n -> p k n", p=P)).then_inc(f.weights_s, 16)
            sp.dma_start(bqkv_sb[:, :], bqkv.partition_broadcast(P)).then_inc(f.weights_s, 16)

            def load_x(j):
                wait(sp, f.ln1.normed_s, j * TT)
                sp.dma_start(f.x_in[:, :, :], tok_tiles(x, j)).then_inc(f.x_loaded_s, 16)

            def store_parts(j):
                sp.wait_ge(part0_s, (j + 1) * TT)
                sp.wait_ge(part1_s, (j + 1) * TT)
                sp.wait_ge(part2_s, (j + 1) * TT)
                dst = qk_dram[bass.ds(j // QC, 1), :, bass.ds((j % QC) * CH, CH)]
                sp.dma_start(dst.rearrange("b (m p) t -> p (b m) t", p=P),
                             parts[:, :, :, :].rearrange("p c m t -> p (c m) t")).then_inc(parts_out_s, 16)

            load_x(0)

            def step(i, front=False, back=False, late=False, ahead=False, load=False):
                if front:
                    wait(sp, f.y_ready_s, i * TT)
                    sp.dma_start(f.x_res[:, :, :], tok_tiles(x, i)).then_inc(f.res_loaded_s, 16)
                if back:
                    wait(sp, roped_s, (i - 1) * TT)
                    sp.dma_start(rope_sb[:, :, :, :], rope[bass.ds((i - 1) * CH, CH), :].rearrange(
                        "(t p) (a d) -> p t a d", p=P, a=2)).then_inc(rope_loaded_s, 16)
                if late:
                    store_parts(i - 2)
                if load:
                    load_x(i + 2)
                if back:
                    sp.wait_ge(v_biased_s, i * TT)
                    sp.dma_start(tok_tiles(v_dram, i - 1), v_sb[:, :, :, :].rearrange("p t h w -> p t (h w)")).then_inc(v_out_s, 16)
                if front:
                    sp.wait_ge(f.y_ready_s, (i + 1) * TT)
                    sp.dma_start(tok_tiles(x2_dram, i), f.y[:, :, :]).then_inc(x2_out_s, 16)
            run(sp, step)
            sp.wait_ge(x2_out_s, CHUNKS * 16)
            sp.wait_ge(parts_out_s, CHUNKS * 16)
            sp.wait_ge(v_out_s, CHUNKS * 16)

        @block.gpsimd
        def _(pool):
            norm_constants(pool, f, consts_s)
            pool.memset(v_sb[:, :, :, :], 1.0).then_inc(consts_s, 1)

            def rope_tile(j, t):
                n = j * TT + t
                src = qk[:, t % 2, :, :]
                cos = rope_sb[:, t, 0:1, :].to_broadcast([P, HQK, HD])
                sin_low = rope_sb[:, t, 1:2, 0:HD // 2].to_broadcast([P, HQK, HD // 2])
                sin_high = rope_sb[:, t, 1:2, HD // 2:HD].to_broadcast([P, HQK, HD // 2])
                pool.wait_ge(qk_biased_s, n + 1)
                if t == 0:
                    pool.wait_ge(rope_loaded_s, (j + 1) * 16)
                wait(pool, roped_s, n)
                pool.tensor_tensor(qk_cos[:, :, :], src, cos, ALU.mult).then_inc(rope_step_s, 1)
                pool.tensor_tensor(qk_sin[:, :, 0:HD // 2], src[:, :, HD // 2:HD], sin_low, ALU.mult).then_inc(rope_step_s, 1)
                pool.tensor_tensor(qk_sin[:, :, HD // 2:HD], src[:, :, 0:HD // 2], sin_high, ALU.mult).then_inc(rope_step_s, 1)
                pool.wait_ge(rope_step_s, 3 * n + 3)
                wait(pool, roped_t_s, n - 1)
                pool.tensor_tensor(qk_rot[:, t % 2, :], qk_cos[:, :, :].rearrange("p h d -> p (h d)"),
                                   qk_sin[:, :, :].rearrange("p h d -> p (h d)"), ALU.add).then_inc(roped_s, 1)

            def last_part(j, t):
                n = j * TT + t
                pool.wait_ge(part1_s, n + 1)
                if t == 0:
                    wait(pool, parts_out_s, j * 16)
                pool.tensor_tensor(parts[:, 2, :, t * P:(t + 1) * P], rest[:, t % 2, :, :],
                                   parts[:, 1, :, t * P:(t + 1) * P], ALU.subtract).then_inc(part2_s, 1)

            def step(i, front=False, back=False, late=False, ahead=False, load=False):
                if ahead:
                    norm_root(pool, f, f.ln1, i + 1)
                if late:
                    last_part(i - 2, TT - 1)
                if back:
                    for t in range(TT):
                        rope_tile(i - 1, t)
                        if t >= 2:
                            last_part(i - 1, t - 2)
                if front:
                    norm_root(pool, f, ln2, i)
                if back:
                    last_part(i - 1, TT - 2)
            run(pool, step)

        @block.tensor
        def _(pe):
            pe.wait_ge(f.split_hi_s, 2 + len(pairs))
            pe.wait_ge(f.split_lo_s, len(pairs))

            def qkv_tile(j, t):
                n = j * TT + t
                if t == 0:
                    pe.wait_ge(x2_hi_s, (j + 1) * KD)
                    pe.wait_ge(x2_lo_s, (j + 1) * KD)
                wait(pe, qk_biased_s, n)
                wait(pe, v_biased_s, n)
                rows = slice(t * P, (t + 1) * P)
                product(pe, qk_bank, lambda c, k: x2nT[c][:, k, rows], lambda c, k: wqkv_sb[c][:, k, 0:2 * D], KD)
                product(pe, v_bank, lambda c, k: x2nT[c][:, k, rows], lambda c, k: wqkv_sb[c][:, k, 2 * D:3 * D],
                        KD).then_inc(qkv_s, 1)

            def turn_tile(j, t, ahead, i):
                n = j * TT + t
                if t < 2 and ahead:
                    pe.wait_ge(f.xn_lo_s, (i + 2) * KD)
                if t >= 2:
                    pe.wait_ge(rest_s, n - 1)
                pe.wait_ge(roped_s, n + 1)
                for c in range(4):
                    last = pe.transpose(f.tr[t % 2][:, c * P:(c + 1) * P], qk_rot[:, t % 2, c * P:(c + 1) * P], f.ident[:, :])
                last.then_inc(roped_t_s, 1)

            def turn_ahead(i, back):
                if back:
                    pe.wait_ge(x2_lo_s, i * KD)
                pe.wait_ge(f.ln1.normed_s, (i + 2) * TT)
                transpose_tokens(pe, f, f.xn).then_inc(f.xn_t_s, 1)

            def step(i, front=False, back=False, late=False, ahead=False, load=False):
                j = i - 1
                for b in range(FB):
                    if front:
                        pe_up(pe, f, i, b)
                    if late and b == 1:
                        turn_tile(j - 1, TT - 1, False, i)
                    if back and b == 3:
                        wait(pe, rest_s, j * TT)
                        pe.wait_ge(ln2.normed_s, (j + 1) * TT)
                        transpose_tokens(pe, f, x2n).then_inc(x2_t_s, 1)
                for t in range(TT):
                    if t == 2 and ahead:
                        turn_ahead(i, back)
                    if back:
                        qkv_tile(j, t)
                    if back and t >= 2:
                        turn_tile(j, t - 2, ahead, i)
                    if front and t == 3 and ahead:
                        pe_logits(pe, f, i + 1)
                    if front:
                        pe_down(pe, f, i, t)
                if ahead:
                    if not front:
                        pe_logits(pe, f, i + 1)
                    pe_turn_logits(pe, f, i + 1)
                if back:
                    turn_tile(j, 2, ahead, i)
            run(pe, step)

        @block.scalar
        def _(act):
            act.wait_ge(f.weights_s, WEIGHTS)
            act_split_weights(act, f, pairs)

            def first_part(j, t):
                act.wait_ge(roped_t_s, j * TT + t + 1)
                if t == 0:
                    wait(act, parts_out_s, j * 16)
                act.activation(parts[:, 0, :, t * P:(t + 1) * P],
                               f.tr[t % 2].rearrange("p (c n) -> p c n", n=P), ACT.Copy).then_inc(part0_s, 1)

            def second_part(j, t):
                act.wait_ge(rest_s, j * TT + t + 1)
                act.activation(parts[:, 1, :, t * P:(t + 1) * P], rest[:, t % 2, :, :], ACT.Copy).then_inc(part1_s, 1)

            def step(i, front=False, back=False, late=False, ahead=False, load=False):
                j = i - 1
                for b in range(FB):
                    if front:
                        act_gelu(act, f, i, b)
                    if late and b == 1:
                        first_part(j - 1, TT - 1)
                        second_part(j - 1, TT - 1)
                    if back and b == 3:
                        act.wait_ge(x2_t_s, j + 1)
                        wait(act, qkv_s, j * TT)
                        for k in range(KD):
                            take_hi(act, f, x2nT, k, x2_hi_s)
                if front:
                    act_router_exp(act, f, i)
                if ahead:
                    act.wait_ge(f.xn_t_s, i + 2)
                    for k in range(KD):
                        take_hi(act, f, f.xnT, k, f.xn_hi_s)
                if back:
                    first_part(j, 0)
                    second_part(j, 0)
                    first_part(j, 1)
                if ahead:
                    act_take_logits(act, f, i + 1)
                if back:
                    second_part(j, 1)
                    first_part(j, 2)
                    second_part(j, 2)
            run(act, step)

        @block.vector
        def _(dve):
            def bias_tile(j, t):
                n = j * TT + t
                dve.wait_ge(qkv_s, n + 1)
                wait(dve, roped_s, n - 1)
                dve.tensor_tensor(qk[:, t % 2, :, :].rearrange("p h d -> p (h d)"), qk_bank,
                                  bqkv_sb[:, 0:2 * D], ALU.add).then_inc(qk_biased_s, 1)
                if t == 0:
                    wait(dve, v_out_s, j * 16)
                dve.tensor_tensor(v_sb[:, t, :, 0:HD], v_bank.rearrange("p (h d) -> p h d", d=HD),
                                  bqkv_sb[:, 2 * D:3 * D].rearrange("p (h d) -> p h d", d=HD),
                                  ALU.add).then_inc(v_biased_s, 1)

            def rest_tile(j, t):
                n = j * TT + t
                dve.wait_ge(part0_s, n + 1)
                wait(dve, part2_s, n - 1)
                dve.tensor_tensor(rest[:, t % 2, :, :], f.tr[t % 2].rearrange("p (c n) -> p c n", n=P),
                                  parts[:, 0, :, t * P:(t + 1) * P], ALU.subtract).then_inc(rest_s, 1)

            def next_stats(i):
                dve.wait_ge(f.x_loaded_s, (i + 2) * 16)
                for t in range(TT):
                    norm_stats(dve, f.ln1, f.x_in, t)

            def next_apply(i, t):
                if t == 0:
                    wait(dve, f.xn_t_s, i + 1)
                norm_apply(dve, f.ln1, f.x_in, f.xn, i + 1, t)

            dve.wait_ge(f.weights_s, WEIGHTS)
            dve_split_weights(dve, f, pairs)
            dve.wait_ge(consts_s, 5)

            def step(i, front=False, back=False, late=False, ahead=False, load=False):
                j = i - 1
                if ahead:
                    next_stats(i)
                if front:
                    dve_gelu_lo(dve, f, i, 0)
                if ahead:
                    norm_moments(dve, f.ln1, i + 1)
                for b in range(1, 4):
                    if front:
                        dve_gelu_lo(dve, f, i, b)
                    if late and b == 1:
                        rest_tile(j - 1, TT - 1)
                if back:
                    wait(dve, qkv_s, j * TT)
                    for k in range(KD):
                        take_lo(dve, f, x2nT, k, j, x2_hi_s, x2_lo_s)
                for t in range(TT):
                    if front:
                        dve_gelu_lo(dve, f, i, 4 + t)
                    if ahead:
                        next_apply(i, t)
                if back:
                    bias_tile(j, 0)
                if front:
                    dve_gate(dve, f, i)
                    dve.wait_ge(f.res_loaded_s, (i + 1) * 16)
                    wait(dve, x2_out_s, i * 16)

                def tile(t):
                    if front:
                        dve_residual(dve, f, i, t, f.x_res)
                        dve.wait_ge(f.y_ready_s, i * TT + t + 1)
                        norm_stats(dve, ln2, f.y, t)
                tile(0)
                if back:
                    bias_tile(j, 1)
                tile(1)
                if ahead:
                    for k in range(KD):
                        take_lo(dve, f, f.xnT, k, i + 1, f.xn_hi_s, f.xn_lo_s)
                if back:
                    bias_tile(j, 2)
                tile(2)
                if back:
                    rest_tile(j, 0)
                    bias_tile(j, 3)
                    rest_tile(j, 1)
                tile(3)
                if ahead:
                    dve_router(dve, f, i + 1)
                if front:
                    norm_moments(dve, ln2, i)
                if back:
                    rest_tile(j, 2)
                if front:
                    wait(dve, x2_t_s, i)
                    for t in range(TT):
                        norm_apply(dve, ln2, f.y, x2n, i, t)
            run(dve, step)



def attention_phase(nc, phase, ident, qk_dram, v_dram, ctx_dram):
    def sb(name, shape, dt=F32):
        return phase.enter_context(nc.sbuf_tensor("b_" + name, shape, dt))

    def sem(name):
        return phase.enter_context(nc.semaphore("b_" + name))

    SLOT = QUAD * SEQ
    ident_f = sb("ident_f", [P, P])
    ident_b = sb("ident_b", [P, P], BF16)
    q_stack = sb("q_stack", [STACK, RING * SLOT], BF16)
    k_stack = sb("k_stack", [STACK, RING * SLOT], BF16)
    v_sb = sb("v", [P, KB, QUAD, VW])
    probs = sb("probs", [P, 2, QUAD, CH])
    ctx_sb = sb("ctx_sb", [P, CH])
    PAIRS = QUAD * TT
    KP = SEQ // CH
    UNITS = PAIRS * KP
    maxes = sb("maxes", [P, PAIRS, KP])
    one = sb("one", [P, PAIRS])
    shift = sb("shift", [P, PAIRS])
    shift_rest = sb("shift_rest", [P, 2, PAIRS])
    shift_parts = sb("shift_parts", [P, P], BF16)
    shift_t = sb("shift_t", [PARTS * PAIRS, P], BF16)
    banks = phase.enter_context(nc.psum_tensor("b_banks", [P, 8, CH], F32))
    acc = banks[:, QUAD, :]
    NM = 3
    PASSES = GROUPS * QC
    TURN = 10
    NU = UNITS + 1

    ident_s = sem("ident")
    ones_s = sem("ones")
    one_s = sem("one")
    stack_s = sem("stack")
    v_s = [sem(f"v{p}") for p in range(4)]
    score_s = sem("score_ready")
    exp_s = sem("exped")
    pv_s = sem("pv_done")
    user_s = sem("max_bank_ready")
    freed_s = sem("max_bank_freed")
    shift_s = sem("shift_ready")
    split_s = sem("split_step")
    parts_s = sem("shift_parts")
    rows_s = sem("shift_rows")
    ctx_s = sem("ctx_ready")
    ctx_out_s = sem("ctx_out")
    LOADS = len(Q_PART) * 2 * 16
    ROWS = PARTS * QUAD * 16

    def bank_of(place):
        return banks[:, QUAD + 1 + place % NM, :]

    def done(n, place):
        if isinstance(n, int) and n == 0:
            return place + 1 if place < TURN else place
        if isinstance(n, int) and n == PASSES:
            return n * NU
        return n * NU + place

    def bank_free(n, place):
        first = isinstance(n, int) and n == 0
        before = [p for p in range(place) if p % NM == place % NM and not (first and p == TURN)]
        if isinstance(n, int) and n == PASSES:
            return n * NU - 1
        if before:
            return done(n, before[-1])
        return 0 if first else done(n - 1, max(p for p in range(NU) if p % NM == place % NM))

    def slot_of(n):
        return ((n // QC) % RING) * SLOT

    def run(eng, step):
        step(0, None)
        with eng.Fori(1, QC) as n:
            step(n, None)
        step(QC, 0)
        with eng.Fori(1, PASSES - QC) as m:
            step(m + QC, m)
        step(PASSES, PASSES - QC)
        for m in range(PASSES - QC + 1, PASSES):
            step(None, m)

    with nc.Block() as block:
        @block.sync
        def _(sp):
            sp.dma_start(ident_f[:, :], ident).then_inc(ident_s, 16)

            def load_stacks(g):
                at = (g % RING) * SLOT
                if not (isinstance(g, int) and g < RING):
                    sp.wait_ge(score_s, (g - RING + 1) * QC * KB * 2)
                wait(sp, stack_s, g * LOADS)
                for r in range(len(Q_PART)):
                    for stack, part, which in ((q_stack, Q_PART[r], 0), (k_stack, K_PART[r], 1)):
                        rows = (g % QC) * (QUAD * HD) + (part * 2 + which) * D
                        src = qk_dram[bass.ds(g // QC, 1), bass.ds(rows, QUAD * HD), :].rearrange("b (j d) t -> d (b j) t", d=HD)
                        dst = stack[HD * r:HD * (r + 1), bass.ds(at, SLOT)].rearrange("p (j t) -> p j t", j=QUAD)
                        sp.dma_start(dst, src).then_inc(stack_s, 16)

            def load_v(g, piece):
                rows, cols = SEQ // 4, QUAD * VW
                src = v_dram[bass.ds((g // QC) * SEQ + piece * rows, rows), bass.ds((g % QC) * cols, cols)]
                sp.dma_start(v_sb[:, 4 * piece:4 * piece + 4, :, :].rearrange("p k h w -> p k (h w)"),
                             src.rearrange("(k p) n -> p k n", p=P)).then_inc(v_s[piece], 16)

            def store_rows(n):
                sp.wait_ge(freed_s, done(n + 1, TURN))
                at = slot_of(n) + (n % QC) * CH
                for c in range(PARTS):
                    for j in range(QUAD):
                        first = c * PAIRS + j * TT
                        sp.dma_start(q_stack[SHIFT_ROW + c:SHIFT_ROW + c + 1, bass.ds(at + j * SEQ, CH)],
                                     shift_t[first:first + TT, :]).then_inc(rows_s, 16)

            def store_ctx(m):
                sp.wait_ge(ctx_s, m + 1)
                dst = ctx_dram[bass.ds(m // QC, 1), :, bass.ds((m % QC) * CH, CH)].rearrange("g p t -> (g p) t")
                sp.dma_start(dst, ctx_sb[:, :]).then_inc(ctx_out_s, 16)

            load_stacks(0)
            for piece in range(4):
                load_v(0, piece)
            store_rows(0)
            load_stacks(1)
            for n in range(1, QC - 1):
                store_rows(n)
            load_stacks(2)

            def chunk(m, g, qc):
                last = isinstance(g, int) and g == GROUPS - 1
                if not last or qc == 0:
                    store_rows(m + QC - 1)
                if not (isinstance(m, int) and m == 0):
                    store_ctx(m - 1)
                if qc == QC - 1 and not last:
                    for piece in range(4):
                        sp.wait_ge(pv_s, m * KB + 4 * piece + 4)
                        load_v(g + 1, piece)

            for qc in range(QC):
                chunk(qc, 0, qc)
            with sp.Fori(1, GROUPS - 2) as g:
                load_stacks(g + 2)
                for qc in range(QC):
                    chunk(g * QC + qc, g, qc)
            for g in (GROUPS - 2, GROUPS - 1):
                for qc in range(QC):
                    chunk(g * QC + qc, g, qc)
            store_ctx(PASSES - 1)
            sp.wait_ge(ctx_out_s, PASSES * 16)

        @block.gpsimd
        def _(pool):
            pool.memset(one[:, :], 1.0).then_inc(one_s, 1)
            pool.wait_ge(one_s, 1)
            pool.memset(k_stack[SR:STACK, :], 1.0).then_inc(ones_s, 1)

            with pool.Fori(0, PASSES) as n:
                pool.wait_ge(shift_s, n + 1)
                pool.tensor_tensor(shift_parts[:, 0 * PAIRS:1 * PAIRS], shift[:, :], one[:, :], ALU.mult).then_inc(split_s, 1)
                pool.wait_ge(split_s, 4 * n + 1)
                pool.tensor_tensor(shift_rest[:, 0, :], shift[:, :], shift_parts[:, 0 * PAIRS:1 * PAIRS], ALU.subtract).then_inc(split_s, 1)
                pool.wait_ge(split_s, 4 * n + 2)
                pool.tensor_tensor(shift_parts[:, 1 * PAIRS:2 * PAIRS], shift_rest[:, 0, :], one[:, :], ALU.mult).then_inc(split_s, 1)
                pool.wait_ge(split_s, 4 * n + 3)
                pool.tensor_tensor(shift_rest[:, 1, :], shift_rest[:, 0, :], shift_parts[:, 1 * PAIRS:2 * PAIRS], ALU.subtract).then_inc(split_s, 1)
                pool.wait_ge(split_s, 4 * n + 4)
                pool.tensor_tensor(shift_parts[:, 2 * PAIRS:3 * PAIRS], shift_rest[:, 1, :], one[:, :], ALU.mult).then_inc(parts_s, 1)

        @block.tensor
        def _(pe):
            pe.wait_ge(ones_s, 3)

            def unit(n, place, slot, at):
                pair, piece = divmod(place - (place > TURN), KP)
                j, tile = divmod(pair, TT)
                wait(pe, freed_s, bank_free(n, place))
                pe.matmul(bank_of(place), q_stack[0:SR, bass.ds(at + (j * SEQ + tile * P), P)],
                          k_stack[0:SR, bass.ds(slot + (j * SEQ + piece * CH), CH)],
                          start=True, stop=True).then_inc(user_s, 1)

            def turn(n):
                pe.wait_ge(parts_s, n)
                pe.wait_ge(freed_s, bank_free(n, TURN))
                pe.transpose(bank_of(TURN)[:, 0:P // 2].bitcast(BF16), shift_parts[:, :], ident_b[:, :]).then_inc(user_s, 1)

            def step(n, m):
                todo = list(range(NU))
                if n is None or (isinstance(n, int) and n == PASSES):
                    todo = [] if n is None else [TURN]
                elif isinstance(n, int) and n == 0:
                    todo.remove(TURN)
                if len(todo) > 1:
                    pe.wait_ge(stack_s, (n // QC + 1) * LOADS)
                    slot = pe.snap(slot_of(n)) if not isinstance(n, int) else slot_of(n)
                    at = pe.snap(slot + (n % QC) * CH) if not isinstance(n, int) else slot + (n % QC) * CH

                def users(count):
                    for _ in range(min(count, len(todo))):
                        place = todo.pop(0)
                        if place == TURN:
                            turn(n)
                        else:
                            unit(n, place, slot, at)

                if m is None:
                    users(NU)
                    return
                pe.wait_ge(rows_s, (m + QC - 1) * ROWS if not isinstance(m, int) else min(m + QC - 1, PASSES) * ROWS)
                kslot = pe.snap(slot_of(m)) if not isinstance(m, int) else slot_of(m)
                qat = pe.snap(kslot + (m % QC) * CH) if not isinstance(m, int) else kslot + (m % QC) * CH

                def scores(kb, half):
                    for j in (2 * half, 2 * half + 1):
                        last = pe.matmul(banks[:, j, :], k_stack[:, bass.ds(kslot + (j * SEQ + kb * P), P)],
                                         q_stack[:, bass.ds(qat + j * SEQ, CH)], start=True, stop=True)
                    last.then_inc(score_s, 1)

                def add_values(kb):
                    if kb == 0:
                        wait(pe, ctx_s, m)
                    if kb % 4 == 0:
                        pe.wait_ge(v_s[kb // 4], (m // QC + 1) * 16)
                    for j in range(QUAD):
                        last = pe.matmul(acc[VW * j:VW * (j + 1), :], v_sb[:, kb, j, :], probs[:, kb % 2, j, :],
                                         start=(kb == 0), stop=(kb == KB - 1))
                    last.then_inc(pv_s, 1)

                for kb in range(KB):
                    s = m * KB + kb
                    wait(pe, exp_s, 2 * s - 1)
                    scores(kb, 0)
                    users(1)
                    wait(pe, exp_s, 2 * s)
                    scores(kb, 1)
                    users(1)
                    if kb:
                        add_values(kb - 1)
                        users(2)
                users(NU)
                pe.wait_ge(exp_s, 2 * (m + 1) * KB)
                add_values(KB - 1)
            run(pe, step)

        @block.scalar
        def _(act):
            act.wait_ge(ident_s, 16)
            act.activation(ident_b[:, :], ident_f[:, :], ACT.Copy).then_inc(ones_s, 1)
            act.activation(shift_parts[:, PARTS * PAIRS:P], ident_f[:, PARTS * PAIRS:P], ACT.Copy, scale=0.0).then_inc(ones_s, 1)

            def step(n, m):
                if m is None:
                    return
                for kb in range(KB):
                    s = m * KB + kb
                    for half in range(2):
                        act.wait_ge(score_s, 2 * s + half + 1)
                        if half == 0:
                            wait(act, pv_s, s - 1)
                        act.activation(probs[:, kb % 2, 2 * half:2 * half + 2, :], banks[:, 2 * half:2 * half + 2, :],
                                       ACT.Exp, scale=SCORE_SCALE).then_inc(exp_s, 1)
                act.wait_ge(pv_s, (m + 1) * KB)
                wait(act, ctx_out_s, m * 16)
                act.activation(ctx_sb[:, :], acc, ACT.Copy).then_inc(ctx_s, 1)
            step(None, 0)
            with act.Fori(1, PASSES) as m:
                step(None, m)

        @block.vector
        def _(dve):
            def turned(n):
                dve.wait_ge(user_s, done(n, TURN))
                wait(dve, rows_s, (n - 1) * ROWS)
                dve.tensor_copy(shift_t[:, :], bank_of(TURN)[0:PARTS * PAIRS, 0:P // 2].bitcast(BF16)).then_inc(freed_s, 1)

            def pass_max(n):
                wait(dve, shift_s, n)
                for place in range(NU):
                    if place == TURN:
                        if not (isinstance(n, int) and n == 0):
                            turned(n)
                        continue
                    pair, piece = divmod(place - (place > TURN), KP)
                    dve.wait_ge(user_s, done(n, place))
                    dve.reduce_max(maxes[:, pair, piece:piece + 1], bank_of(place), axis=X).then_inc(freed_s, 1)
                dve.wait_ge(freed_s, done(n, NU - 1))
                wait(dve, parts_s, n)
                dve.tensor_reduce(shift[:, :], maxes[:, :, :], X, ALU.max, negate=True).then_inc(shift_s, 1)
            pass_max(0)
            pass_max(1)
            with dve.Fori(2, PASSES) as n:
                pass_max(n)
            turned(PASSES)



def output_phase(nc, phase, wo, bo, router, w1, b1, w2, b2, ident, x2_dram, ctx_dram, out):
    sb, sem = allocators(nc, phase, "c_")
    f = ffn_buffers(nc, phase, "c_")
    wo_raw = sb("wo_raw", [P, KD, D])
    wo_sb = split_pair(sb, "wo", [P, KD, D])
    bo_sb = sb("bo", [P, D])
    x2_sb = sb("x2", [P, TT, D])
    raw = sb("raw", [P, QUAD, CH])
    sum_rec = sb("sum_rec", [P, 2, HEADS])
    context = sb("context", [P, TT, D])
    contextT = split_pair(sb, "contextT", [P, KD, CH])
    projected = sb("projected", [P, TT, D])
    proj_banks = [f.banks[:, 6 + k, 0:D] for k in range(2)]

    consts_s = sem("consts")
    raw_loaded_s = sem("raw_loaded")
    x2_loaded_s = sem("x2_loaded")
    raw_t_s = sem("raw_t")
    sum_rec_s = sem("sum_rec")
    context_s = sem("context_ready")
    context_t_s = sem("context_t")
    context_hi_s = sem("context_hi")
    context_lo_s = sem("context_lo")
    proj_s = sem("proj")
    proj_bias_s = sem("proj_bias")
    x3_s = sem("x3")
    out_s = sem("out")
    WEIGHTS = FFN_WEIGHTS + 2 * 16
    pairs = ffn_pairs(f) + [(wo_raw, wo_sb, D)]

    def run(eng, step):
        step(-1, ahead=True, load=True)
        step(0, front=True, ahead=True, load=True)
        with eng.Fori(1, CHUNKS - 2) as i:
            step(i, front=True, ahead=True, load=True)
        step(CHUNKS - 2, front=True, ahead=True)
        step(CHUNKS - 1, front=True)

    with nc.Block() as block:
        @block.sync
        def _(sp):
            def load_raw(j):
                wait(sp, raw_t_s, j * TT)
                sp.dma_start(raw[:, :, :], ctx_dram[bass.ds((j // QC) * QUAD, QUAD), :, bass.ds((j % QC) * CH, CH)].rearrange(
                    "g p t -> p g t")).then_inc(raw_loaded_s, 16)

            def load_x2(j):
                wait(sp, x3_s, j * TT)
                sp.dma_start(x2_sb[:, :, :], tok_tiles(x2_dram, j)).then_inc(x2_loaded_s, 16)

            def step(i, front=False, ahead=False, load=False):
                if load:
                    load_raw(i + 2)
                    load_x2(i + 2)
                if front:
                    sp.wait_ge(f.y_ready_s, (i + 1) * TT)
                    sp.dma_start(tok_tiles(out, i), f.y[:, :, :]).then_inc(out_s, 16)
            load_ffn_weights(sp, f, router, w1, b1, w2, b2, ident)
            sp.dma_start(wo_raw[:, :, :], wo.rearrange("(k p) n -> p k n", p=P)).then_inc(f.weights_s, 16)
            sp.dma_start(bo_sb[:, :], bo.partition_broadcast(P)).then_inc(f.weights_s, 16)
            load_raw(0)
            load_x2(0)
            run(sp, step)
            sp.wait_ge(out_s, CHUNKS * 16)

        @block.gpsimd
        def _(pool):
            norm_constants(pool, f, consts_s)

            def step(i, front=False, ahead=False, load=False):
                if ahead:
                    norm_root(pool, f, f.ln1, i + 1)
                    wait(pool, f.y_ready_s, (i + 1) * TT)
                    pool.wait_ge(x3_s, (i + 2) * TT)
                    pool.tensor_tensor(f.x_res[:, :, :], f.x_in[:, :, :],
                                       f.consts[:, 3, :].unsqueeze(2).to_broadcast([P, TT, D]), ALU.mult).then_inc(f.res_copied_s, 1)
            run(pool, step)

        @block.tensor
        def _(pe):
            pe.wait_ge(f.split_hi_s, 2 + len(pairs))
            pe.wait_ge(f.split_lo_s, len(pairs))

            def turn_raw(j, t):
                if t == 0:
                    pe.wait_ge(raw_loaded_s, (j + 1) * 16)
                if t < 2:
                    wait(pe, f.xn_lo_s, j * KD)
                else:
                    pe.wait_ge(context_s, j * TT + t - 1)
                for g in range(QUAD):
                    last = pe.transpose(f.tr[t % 2][:, g * P:(g + 1) * P], raw[:, g, t * P:(t + 1) * P], f.ident[:, :])
                last.then_inc(raw_t_s, 1)

            def turn_context(j):
                pe.wait_ge(context_s, (j + 1) * TT)
                transpose_tokens(pe, f, context).then_inc(context_t_s, 1)

            def project(j, t):
                if t == 0:
                    pe.wait_ge(context_hi_s, (j + 1) * KD)
                    pe.wait_ge(context_lo_s, (j + 1) * KD)
                wait(pe, proj_bias_s, j * TT + t - 1)
                product(pe, proj_banks[t % 2], lambda c, k: contextT[c][:, k, t * P:(t + 1) * P],
                        lambda c, k: wo_sb[c][:, k, :], KD).then_inc(proj_s, 1)

            def turn_ahead(j):
                pe.wait_ge(f.ln1.normed_s, (j + 1) * TT)
                transpose_tokens(pe, f, f.xn).then_inc(f.xn_t_s, 1)

            def step(i, front=False, ahead=False, load=False):
                j = i + 1
                for b in range(FB):
                    if front:
                        pe_up(pe, f, i, b)
                    if ahead and b in (1, 2, 3, 4):
                        turn_raw(j, b - 1)
                    if ahead and b == 6:
                        turn_context(j)
                if ahead:
                    for t in range(TT):
                        project(j, t)
                if front:
                    for t in range(3):
                        pe_down(pe, f, i, t)
                if ahead:
                    turn_ahead(j)
                if front:
                    pe_down(pe, f, i, 3)
                if ahead:
                    pe_logits(pe, f, j)
                    pe_turn_logits(pe, f, j)
            run(pe, step)

        @block.scalar
        def _(act):
            act.wait_ge(f.weights_s, WEIGHTS)
            act_split_weights(act, f, pairs)

            def step(i, front=False, ahead=False, load=False):
                j = i + 1
                if front:
                    for b in range(FB - 1):
                        act_gelu(act, f, i, b)
                if ahead:
                    act.wait_ge(context_t_s, j + 1)
                    wait(act, proj_s, j * TT)
                    for k in range(KD):
                        take_hi(act, f, contextT, k, context_hi_s)
                if front:
                    act_gelu(act, f, i, FB - 1)
                    act_router_exp(act, f, i)
                if ahead:
                    act.wait_ge(f.xn_t_s, j + 1)
                    for k in range(KD):
                        take_hi(act, f, f.xnT, k, f.xn_hi_s)
                    act_take_logits(act, f, j)
            run(act, step)

        @block.vector
        def _(dve):
            dve.wait_ge(f.weights_s, WEIGHTS)
            dve_split_weights(dve, f, pairs)

            def divide(j, t):
                n = j * TT + t
                raw_t = f.tr[t % 2].rearrange("p (h w) -> p h w", w=VW)
                dve.wait_ge(raw_t_s, n + 1)
                if t == 0:
                    wait(dve, context_t_s, j)
                dve.reciprocal(sum_rec[:, t % 2, :].unsqueeze(2), raw_t[:, :, HD:HD + 1]).then_inc(sum_rec_s, 1)
                dve.wait_ge(sum_rec_s, n + 1)
                dve.tensor_tensor(context[:, t, :].rearrange("p (h d) -> p h d", d=HD), raw_t[:, :, 0:HD],
                                  sum_rec[:, t % 2, :].unsqueeze(2).to_broadcast([P, HEADS, HD]), ALU.mult).then_inc(context_s, 1)

            def add_output(j, t):
                n = j * TT + t
                dve.wait_ge(proj_s, n + 1)
                if t == 0:
                    dve.wait_ge(x2_loaded_s, (j + 1) * 16)
                    wait(dve, f.res_copied_s, j)
                dve.tensor_tensor(projected[:, t, :], proj_banks[t % 2], bo_sb[:, :], ALU.add).then_inc(proj_bias_s, 1)
                dve.wait_ge(proj_bias_s, n + 1)
                dve.tensor_tensor(f.x_in[:, t, :], projected[:, t, :], x2_sb[:, t, :], ALU.add).then_inc(x3_s, 1)

            def step(i, front=False, ahead=False, load=False):
                j = i + 1
                for b in range(FB):
                    if front:
                        dve_gelu_lo(dve, f, i, b) if b < FB - 1 else None
                    if ahead and b in (1, 2, 3, 4):
                        divide(j, b - 1)
                if ahead:
                    wait(dve, proj_s, j * TT)
                    for k in range(KD):
                        take_lo(dve, f, contextT, k, j, context_hi_s, context_lo_s)
                if front:
                    dve_gelu_lo(dve, f, i, FB - 1)
                    dve_gate(dve, f, i)
                if ahead:
                    for t in range(TT):
                        add_output(j, t)
                        dve.wait_ge(x3_s, j * TT + t + 1)
                        norm_stats(dve, f.ln1, f.x_in, t)
                    norm_moments(dve, f.ln1, j)
                if front:
                    dve.wait_ge(f.res_copied_s, i + 1)
                    wait(dve, out_s, i * 16)
                    for t in range(2):
                        dve_residual(dve, f, i, t, f.x_res)
                if ahead:
                    wait(dve, f.xn_t_s, j)
                    for t in range(TT):
                        norm_apply(dve, f.ln1, f.x_in, f.xn, j, t)
                if front:
                    dve_residual(dve, f, i, 2, f.x_res)
                if ahead:
                    for k in range(KD):
                        take_lo(dve, f, f.xnT, k, j, f.xn_hi_s, f.xn_lo_s)
                if front:
                    dve_residual(dve, f, i, 3, f.x_res)
                if ahead:
                    dve_router(dve, f, j)
            run(dve, step)


def rope_table():
    import numpy as np

    half = HD // 2
    inv = (np.float32(1.0) / np.power(np.float32(10000.0), np.arange(half, dtype=np.float32) / np.float32(half))).astype(np.float32)
    angle = np.outer(np.arange(SEQ, dtype=np.float32), inv).astype(np.float32)
    cos, sin = np.cos(angle), np.sin(angle)
    table = np.concatenate([cos, cos, -sin, sin], axis=1).astype(np.float32)
    return np.tile(table, (BATCH, 1))


def kernel(**inputs):
    import numpy as np
    from concourse import bacc
    from concourse.bass_utils import run_bass_kernel_spmd

    a = {name: np.asarray(value) for name, value in inputs.items()}
    arrays = {
        "x": a["L0_attn_x"].reshape(TOKENS, D),
        "wqkv": np.concatenate([a["L0_attn_Wq"].T, a["L0_attn_Wk"].T, a["L0_attn_Wv"].T], axis=1),
        "bqkv": np.concatenate([a["L0_attn_bq"], a["L0_attn_bk"], a["L0_attn_bv"]]).reshape(1, 3 * D),
        "wo": a["L0_attn_Wo"].T,
        "bo": a["L0_attn_bo"].reshape(1, D),
        "router": a["L0_ffn_router_w"],
        "w1": a["L0_ffn_w1"],
        "b1": a["L0_ffn_b1"].reshape(FB, P).T,
        "w2": a["L0_ffn_w2"],
        "b2": a["L0_ffn_b2"].reshape(1, D),
        "rope": rope_table(),
        "ident": np.eye(P, dtype=np.float32),
    }
    arrays = {name: np.ascontiguousarray(value) for name, value in arrays.items()}
    nc = bacc.Bacc("TRN2", target_bir_lowering=False, num_devices=1)
    ins = [nc.dram_tensor(name, v.shape, mybir.dt.from_np(v.dtype), kind="ExternalInput").ap() for name, v in arrays.items()]
    out = nc.dram_tensor("out", (TOKENS, D), F32, kind="ExternalOutput").ap()
    build(nc, *ins, out)
    got = run_bass_kernel_spmd(nc, [arrays], core_ids=[0])
    return got.results[0]["out"].reshape(BATCH, SEQ, D)
```

```python
from contextlib import ExitStack

import concourse.bass as bass
from concourse import mybir

ALU = mybir.AluOpType
ACT = mybir.ActivationFunctionType
F32 = mybir.dt.float32
BF16 = mybir.dt.bfloat16
F32R = mybir.dt.float32r
X = mybir.AxisListType.X

P = 128
BATCH, SEQ, D = 4, 2048, 256
HEADS, HD = 16, 16
FF, EXPERTS, TOP_K = 1024, 8, 2
TOKENS = BATCH * SEQ
EPS = 1e-5

KD = D // P
FB = FF // P
CH = 512
TT = CH // P
CHUNKS = TOKENS // CH

QUAD = 4
GROUPS = BATCH * HEADS // QUAD
QC = SEQ // CH
KB = SEQ // P
VW = 32
PARTS = 3
Q_PART = (0, 0, 0, 1, 1, 2)
K_PART = (0, 1, 2, 0, 1, 0)
SR = HD * len(Q_PART)
SHIFT_ROW = SR
STACK = SR + PARTS
RING = 3
SCORE_SCALE = HD ** -0.5


def wait(eng, sem, value):
    if not (isinstance(value, int) and value <= 0):
        eng.wait_ge(sem, value)


def build(nc, x, wqkv, bqkv, wo, bo, router, w1, b1, w2, b2, rope, ident, out):
    ctx = ExitStack()
    with ctx:
        x2_dram = nc.dram_tensor("x2_dram", (TOKENS, D), F32, kind="Internal").ap()
        qk_dram = nc.dram_tensor("qk_dram", (BATCH, PARTS * 2 * D, SEQ), BF16, kind="Internal").ap()
        v_dram = nc.dram_tensor("v_dram", (TOKENS, HEADS * VW), F32, kind="Internal").ap()
        ctx_dram = nc.dram_tensor("ctx_dram", (GROUPS, P, SEQ), F32, kind="Internal").ap()
        w = resident_weights(nc, ctx)
        with ExitStack() as phase:
            project_phase(nc, phase, w, x, wqkv, bqkv, wo, bo, router, w1, b1, w2, b2, rope, ident, x2_dram, qk_dram, v_dram)
        with ExitStack() as phase:
            attention_phase(nc, phase, w, qk_dram, v_dram, ctx_dram)
        with ExitStack() as phase:
            output_phase(nc, phase, w, x2_dram, ctx_dram, out)


def tok_tiles(ap, chunk):
    return ap[bass.ds(chunk * CH, CH), :].rearrange("(t p) n -> p t n", p=P)



class Buffers:
    pass


def allocators(nc, phase, pre):
    def sb(name, shape, dt=F32):
        return phase.enter_context(nc.sbuf_tensor(pre + name, shape, dt))

    def sem(name):
        return phase.enter_context(nc.semaphore(pre + name))
    return sb, sem


def split_pair(sb, name, shape):
    return sb(name + "_hi", shape, F32R), sb(name + "_lo", shape, F32R)


def resident_weights(nc, ctx):
    sb, sem = allocators(nc, ctx, "w_")
    w = Buffers()
    w.w1 = split_pair(sb, "w1", [P, KD, FF])
    w.w2 = split_pair(sb, "w2", [P, FB, D])
    w.router = split_pair(sb, "router", [P, KD, P])
    w.wo = split_pair(sb, "wo", [P, KD, D])
    w.b1 = sb("b1", [P, FB])
    w.b2 = sb("b2", [P, D])
    w.bo = sb("bo", [P, D])
    w.ident = sb("ident", [P, P])
    w.consts = sb("consts", [P, 4, TT])
    return w


def ffn_buffers(nc, phase, pre, w):
    sb, sem = allocators(nc, phase, pre)
    f = Buffers()
    f.w1, f.w2, f.router, f.b1, f.b2, f.ident, f.consts = w.w1, w.w2, w.router, w.b1, w.b2, w.ident, w.consts
    f.table = sb("table", [P, 1])
    f.x_in = sb("x_in", [P, TT, D])
    f.x_res = sb("x_res", [P, TT, D])
    f.xn = sb("xn", [P, TT, D])
    f.xnT = split_pair(sb, "xnT", [P, KD, CH])
    f.hidden = sb("hidden", [P, 2, CH])
    f.hT = split_pair(sb, "hT", [P, FB, CH])
    f.logitsT = sb("logitsT", [P, CH])
    f.ffn_out = sb("ffn_out", [P, TT, D])
    f.y = sb("y", [P, TT, D])
    f.top = sb("top", [P, TT, EXPERTS])
    f.top_max = sb("top_max", [P, TT])
    f.top_shift = sb("top_shift", [P, TT, EXPERTS])
    f.top_exp = sb("top_exp", [P, TT, EXPERTS])
    f.exp_sum = sb("exp_sum", [P, TT])
    f.exp_rec = sb("exp_rec", [P, TT])
    f.top_prob = sb("top_prob", [P, TT, TOP_K])
    f.top_sum = sb("top_sum", [P, TT])
    f.top_rec = sb("top_rec", [P, TT])
    f.combine = sb("combine", [P, TT, TOP_K])
    f.gate = sb("gate", [P, TT])
    f.gate_half = sb("gate_half", [P, TT])
    f.banks = phase.enter_context(nc.psum_tensor(pre + "banks", [P, 8, CH], F32))
    f.tr = [f.banks[:, k, :] for k in range(2)]
    f.up = [f.banks[:, 2 + k, :] for k in range(2)]
    f.down = [f.banks[:, 4 + k, 0:D] for k in range(2)]
    f.logits = f.tr[1].rearrange("p (t e) -> p t e", e=P)[:, :, 0:EXPERTS]
    f.x_loaded_s = sem("x_loaded")
    f.res_loaded_s = sem("res_loaded")
    f.res_copied_s = sem("res_copied")
    f.xn_t_s = sem("xn_t")
    f.xn_hi_s = sem("xn_hi")
    f.xn_lo_s = sem("xn_lo")
    f.up_s = sem("up")
    f.h_hi_s = sem("h_hi")
    f.h_s = sem("h")
    f.h_lo_s = sem("h_lo")
    f.down_s = sem("down")
    f.logits_t_s = sem("logits_t")
    f.logits_taken_s = sem("logits_taken")
    f.logits_s = sem("logits")
    f.top_max_s = sem("top_max")
    f.top_s = sem("top")
    f.shifted_s = sem("shifted")
    f.exped_s = sem("exped")
    f.gate_step_s = sem("gate_step")
    f.half_s = sem("half")
    f.ffn_sum_s = sem("ffn_sum")
    f.y_ready_s = sem("y_ready")
    f.ln1 = norm_buffers(nc, phase, pre + "ln1_")
    return f


def norm_buffers(nc, phase, pre):
    sb, sem = allocators(nc, phase, pre)
    n = Buffers()
    n.stats = sb("stats", [P, TT, 6])
    n.moments = sb("moments", [P, TT, 2])
    n.fence = sb("fence", [P, 1])
    n.var = sb("var", [P, TT])
    n.guess = sb("guess", [P, TT])
    n.square = sb("square", [P, TT])
    n.product = sb("product", [P, TT])
    n.half = sb("half", [P, TT])
    n.factor = sb("factor", [P, TT])
    n.rstd = sb("rstd", [P, TT])
    n.stats_s = sem("stats_s")
    n.moments_s = sem("moments_s")
    n.root_step_s = sem("root_step_s")
    n.rstd_s = sem("rstd_s")
    n.normed_s = sem("normed_s")
    return n


def product(pe, out, left, right, blocks):
    n = 0
    for k in range(blocks):
        for a, b in ((0, 0), (0, 1), (1, 0)):
            last = pe.matmul(out, left(a, k), right(b, k), start=(n == 0), stop=(n == 3 * blocks - 1))
            n += 1
    return last


def norm_stats(dve, n, src, t):
    dve.bn_stats(n.stats[:, t, :], src[:, t, :]).then_inc(n.stats_s, 1)


def norm_moments(dve, n, i):
    dve.wait_ge(n.stats_s, (i + 1) * TT)
    dve.tensor_copy(n.fence[:, :], n.stats[:, TT - 1, 0:1])
    for t in range(TT):
        dve.bn_aggr(n.moments[:, t, :], n.stats[:, t, :]).then_inc(n.moments_s, 1)


def norm_apply(dve, n, src, dst, i, t):
    dve.wait_ge(n.rstd_s, i + 1)
    dve.tensor_scalar(dst[:, t, :], src[:, t, :], n.moments[:, t, 0:1], n.rstd[:, t:t + 1],
                      ALU.subtract, ALU.mult).then_inc(n.normed_s, 1)


ROOT_STEPS = 6


def norm_constants(pool, f, consts_s):
    for k, value in enumerate((EPS, -0.5, 1.5, 1.0)):
        pool.memset(f.consts[:, k, :], value).then_inc(consts_s, 1)
    pool.wait_ge(consts_s, 4)


def norm_root(pool, f, n, i):
    eps, minus_half, three_halves = (f.consts[:, k, :] for k in range(3))
    steps = (
        (n.var, n.moments[:, :, 1], eps, ALU.add),
        (n.guess, n.var[:, :], minus_half, ALU.pow),
        (n.square, n.guess[:, :], n.guess[:, :], ALU.mult),
        (n.product, n.square[:, :], n.var[:, :], ALU.mult),
        (n.half, n.product[:, :], minus_half, ALU.mult),
        (n.factor, n.half[:, :], three_halves, ALU.add),
    )
    pool.wait_ge(n.moments_s, i * TT + TT)
    wait(pool, n.normed_s, i * TT)
    for k, (dst, in0, in1, op) in enumerate(steps):
        if k:
            pool.wait_ge(n.root_step_s, i * ROOT_STEPS + k)
        pool.tensor_tensor(dst[:, :], in0, in1, op).then_inc(n.root_step_s, 1)
    pool.wait_ge(n.root_step_s, i * ROOT_STEPS + ROOT_STEPS)
    pool.tensor_tensor(n.rstd[:, :], n.guess[:, :], n.factor[:, :], ALU.mult).then_inc(n.rstd_s, 1)


def transpose_tokens(pe, f, src):
    for k in range(KD):
        for t in range(TT):
            last = pe.transpose(f.tr[k][:, t * P:(t + 1) * P], src[:, t, k * P:(k + 1) * P], f.ident[:, :])
    return last


def take_hi(act, f, dst, k, sem):
    act.activation(dst[0][:, k, :], f.tr[k], ACT.Copy).then_inc(sem, 1)


def take_lo(dve, f, dst, k, i, hi_s, lo_s):
    dve.wait_ge(hi_s, i * KD + k + 1)
    dve.tensor_tensor(dst[1][:, k, :], f.tr[k], dst[0][:, k, :].bitcast(F32), ALU.subtract).then_inc(lo_s, 1)


def pe_up(pe, f, i, b):
    if b == 0:
        pe.wait_ge(f.xn_hi_s, (i + 1) * KD)
        pe.wait_ge(f.xn_lo_s, (i + 1) * KD)
    wait(pe, f.h_s, i * FB + b - 1)
    product(pe, f.up[b % 2], lambda c, k: f.w1[c][:, k, b * P:(b + 1) * P],
            lambda c, k: f.xnT[c][:, k, :], KD).then_inc(f.up_s, 1)


def pe_logits(pe, f, i):
    pe.wait_ge(f.xn_hi_s, (i + 1) * KD)
    pe.wait_ge(f.xn_lo_s, (i + 1) * KD)
    wait(pe, f.h_s, i * FB)
    product(pe, f.up[1], lambda c, k: f.router[c][:, k, :], lambda c, k: f.xnT[c][:, k, :], KD).then_inc(f.logits_t_s, 1)


def pe_turn_logits(pe, f, i):
    pe.wait_ge(f.logits_taken_s, i + 1)
    for t in range(TT):
        last = pe.transpose(f.tr[1][:, t * P:(t + 1) * P], f.logitsT[:, t * P:(t + 1) * P], f.ident[:, :])
    last.then_inc(f.logits_s, 1)


def pe_down(pe, f, i, t):
    if t == 0:
        pe.wait_ge(f.h_hi_s, (i + 1) * FB)
        pe.wait_ge(f.h_lo_s, (i + 1) * FB)
    wait(pe, f.ffn_sum_s, i * TT + t - 1)
    product(pe, f.down[t % 2], lambda c, k: f.hT[c][:, k, t * P:(t + 1) * P],
            lambda c, k: f.w2[c][:, k, :], FB).then_inc(f.down_s, 1)


def act_fetch_gelu(act, f):
    act.activation(f.table[:, :], f.b1[:, 0:1], ACT.Gelu_apprx_tanh)


def act_gelu(act, f, i, b):
    act.wait_ge(f.up_s, i * FB + b + 1)
    if b == 0:
        wait(act, f.down_s, i * TT)
    act.activation(f.hT[0][:, b, :], f.up[b % 2], ACT.Gelu_apprx_tanh, bias=f.b1[:, b:b + 1]).then_inc(f.h_hi_s, 1)
    wait(act, f.h_lo_s, i * FB + b - 1)
    act.activation(f.hidden[:, b % 2, :], f.up[b % 2], ACT.Gelu_apprx_tanh, bias=f.b1[:, b:b + 1]).then_inc(f.h_s, 1)


def dve_gelu_lo(dve, f, i, b):
    dve.wait_ge(f.h_s, i * FB + b + 1)
    if b == 0:
        wait(dve, f.down_s, i * TT)
    dve.tensor_tensor(f.hT[1][:, b, :], f.hidden[:, b % 2, :], f.hT[0][:, b, :].bitcast(F32),
                      ALU.subtract).then_inc(f.h_lo_s, 1)


def act_take_logits(act, f, i):
    act.wait_ge(f.logits_t_s, i + 1)
    wait(act, f.logits_s, i)
    act.activation(f.logitsT[:, :], f.up[1], ACT.Copy).then_inc(f.logits_taken_s, 1)


def act_router_exp(act, f, i):
    act.wait_ge(f.shifted_s, i + 1)
    wait(act, f.gate_step_s, i * GATE_STEPS)
    act.activation(f.top_exp[:, :, :], f.top_shift[:, :, :], ACT.Exp).then_inc(f.exped_s, 1)


def dve_router(dve, f, i):
    dve.wait_ge(f.logits_s, i + 1)
    dve.reduce_max(f.top_max[:, :], f.logits, axis=X).then_inc(f.top_max_s, 1)
    for t in range(TT):
        dve.max(f.top[:, t, :], f.logits[:, t, :]).then_inc(f.top_s, 1)
    dve.wait_ge(f.top_max_s, i + 1)
    dve.wait_ge(f.top_s, (i + 1) * TT)
    wait(dve, f.exped_s, i)
    dve.tensor_tensor(f.top_shift[:, :, :], f.top[:, :, :], f.top_max[:, :].unsqueeze(2).to_broadcast([P, TT, EXPERTS]),
                      ALU.subtract).then_inc(f.shifted_s, 1)


GATE_STEPS = 7


def dve_gate(dve, f, i):
    s, base = f.gate_step_s, i * GATE_STEPS
    dve.wait_ge(f.exped_s, i + 1)
    dve.reduce_sum(f.exp_sum[:, :], f.top_exp[:, :, :], axis=X).then_inc(s, 1)
    dve.wait_ge(s, base + 1)
    dve.reciprocal(f.exp_rec[:, :], f.exp_sum[:, :]).then_inc(s, 1)
    dve.wait_ge(s, base + 2)
    dve.tensor_tensor(f.top_prob[:, :, :], f.top_exp[:, :, 0:TOP_K],
                      f.exp_rec[:, :].unsqueeze(2).to_broadcast([P, TT, TOP_K]), ALU.mult).then_inc(s, 1)
    dve.wait_ge(s, base + 3)
    dve.reduce_sum(f.top_sum[:, :], f.top_prob[:, :, :], axis=X).then_inc(s, 1)
    dve.wait_ge(s, base + 4)
    dve.reciprocal(f.top_rec[:, :], f.top_sum[:, :]).then_inc(s, 1)
    dve.wait_ge(s, base + 5)
    dve.tensor_tensor(f.combine[:, :, :], f.top_prob[:, :, :],
                      f.top_rec[:, :].unsqueeze(2).to_broadcast([P, TT, TOP_K]), ALU.mult).then_inc(s, 1)
    dve.wait_ge(s, base + 6)
    dve.reduce_sum(f.gate[:, :], f.combine[:, :, :], axis=X).then_inc(s, 1)
    dve.wait_ge(s, base + 7)
    dve.tensor_scalar(f.gate_half[:, :], f.gate[:, :], 0.5, None, ALU.mult).then_inc(f.half_s, 1)


def dve_residual(dve, f, i, t, res):
    dve.wait_ge(f.down_s, i * TT + t + 1)
    dve.tensor_tensor(f.ffn_out[:, t, :], f.down[t % 2], f.b2[:, :], ALU.add).then_inc(f.ffn_sum_s, 1)
    if t == 0:
        dve.wait_ge(f.half_s, i + 1)
    dve.wait_ge(f.ffn_sum_s, i * TT + t + 1)
    dve.scalar_tensor_tensor(f.y[:, t, :], f.ffn_out[:, t, :], f.gate_half[:, t:t + 1], res[:, t, :],
                             ALU.mult, ALU.add).then_inc(f.y_ready_s, 1)



def project_phase(nc, phase, w, x, wqkv, bqkv, wo, bo, router, w1, b1, w2, b2, rope, ident, x2_dram, qk_dram, v_dram):
    sb, sem = allocators(nc, phase, "a_")
    f = ffn_buffers(nc, phase, "a_", w)
    ln2 = norm_buffers(nc, phase, "a_ln2_")
    HQK = 2 * HEADS
    wqkv_sb = split_pair(sb, "wqkv", [P, KD, 3 * D])
    bqkv_sb = sb("bqkv", [P, 3 * D])
    x2n = sb("x2n", [P, TT, D])
    x2nT = split_pair(sb, "x2nT", [P, KD, CH])
    rope_sb = sb("rope_sb", [P, TT, 2, HD])
    qk = sb("qk", [P, 2, HQK, HD])
    qk_cos = sb("qk_cos", [P, 2, HQK, HD])
    qk_sin = sb("qk_sin", [P, HQK, HD])
    qk_rot = sb("qk_rot", [P, 2, HQK * HD])
    rest = sb("rest", [P, 2, 4, P])
    parts = sb("parts", [P, PARTS, 4, CH], BF16)
    v_sb = sb("v_sb", [P, TT, HEADS, VW])
    qk_bank = f.banks[:, 6, :]
    v_bank = f.banks[:, 7, 0:D]

    consts_s = sem("consts")
    rope_loaded_s = sem("rope_loaded")
    x2_t_s = sem("x2_t")
    x2_hi_s = sem("x2_hi")
    x2_lo_s = sem("x2_lo")
    qkv_s = sem("qkv")
    qk_biased_s = sem("qk_biased")
    v_biased_s = sem("v_biased")
    cos_s = sem("cos")
    rope_step_s = sem("rope_step")
    roped_s = sem("roped")
    roped_t_s = sem("roped_t")
    part0_s = sem("part0")
    rest_s = sem("rest_ready")
    part1_s = sem("part1")
    part1_late_s = sem("part1_late")
    part2_s = sem("part2")
    x2_out_s = sem("x2_out")
    parts_out_s = sem("parts_out")
    v_out_s = sem("v_out")
    room = parts[:, :, :, :].rearrange("p c m t -> p (c m t)").bitcast(F32)
    router_raw = sb("router_raw", [P, KD, EXPERTS])
    w1_raw = sb("w1_raw", [P, KD, FF])[:, :, :]
    w2_raw = room[:, 0:FB * D].rearrange("p (k n) -> p k n", k=FB)
    wqkv_raw = sb("wqkv_raw", [P, KD, 3 * D])[:, :, :]
    wo_raw = room[:, FB * D:FB * D + KD * D].rearrange("p (k n) -> p k n", k=KD)
    ROUTER, W1, W2, WQKV, WO = range(5)
    weights = (
        (router, router_raw[:, :, :], w.router, EXPERTS),
        (w1, w1_raw, w.w1, FF),
        (w2, w2_raw, w.w2, D),
        (wqkv, wqkv_raw, wqkv_sb, 3 * D),
        (wo, wo_raw, w.wo, D),
    )
    loaded_s = [sem(f"loaded_{name}") for name in ("router", "w1", "w2", "wqkv", "wo")]
    ident_s = sem("ident")
    biases_s = sem("biases")
    zeros_s = sem("zeros")
    split_hi_s = sem("split_hi")
    split_lo_s = sem("split_lo")

    def act_split(act, k):
        _, raw, (hi, lo), cols = weights[k]
        act.wait_ge(loaded_s[k], 16)
        act.activation(hi[:, :, 0:cols], raw, ACT.Copy).then_inc(split_hi_s, 1)

    def dve_split(dve, k):
        _, raw, (hi, lo), cols = weights[k]
        dve.wait_ge(loaded_s[k], 16)
        dve.wait_ge(split_hi_s, k + 1)
        dve.tensor_tensor(lo[:, :, 0:cols], raw, hi[:, :, 0:cols].bitcast(F32), ALU.subtract).then_inc(split_lo_s, 1)

    def run(eng, step):
        step(-1, ahead=True, load=True)
        step(0, front=True, ahead=True, load=True)
        step(1, front=True, back=True, ahead=True, load=True)
        with eng.Fori(2, CHUNKS - 2) as i:
            step(i, front=True, back=True, late=True, ahead=True, load=True)
        step(CHUNKS - 2, front=True, back=True, late=True, ahead=True)
        step(CHUNKS - 1, front=True, back=True, late=True)
        step(CHUNKS, back=True, late=True)
        step(CHUNKS + 1, late=True)

    with nc.Block() as block:
        @block.sync
        def _(sp):
            def load_x(j):
                wait(sp, f.ln1.normed_s, j * TT)
                sp.dma_start(f.x_in[:, :, :], tok_tiles(x, j)).then_inc(f.x_loaded_s, 16)

            def store_parts(j):
                sp.wait_ge(part2_s, (j + 1) * TT)
                dst = qk_dram[bass.ds(j // QC, 1), :, bass.ds((j % QC) * CH, CH)]
                sp.dma_start(dst.rearrange("b (m p) t -> p (b m) t", p=P),
                             parts[:, :, :, :].rearrange("p c m t -> p (c m) t")).then_inc(parts_out_s, 16)

            load_x(0)
            sp.dma_start(w.ident[:, :], ident).then_inc(ident_s, 16)
            for k, (src, raw, _, _) in enumerate(weights):
                sp.dma_start(raw, src.rearrange("(k p) n -> p k n", p=P)).then_inc(loaded_s[k], 16)
                if k == W1:
                    sp.dma_start(w.b1[:, :], b1).then_inc(biases_s, 16)
                    sp.dma_start(w.b2[:, :], b2.partition_broadcast(P)).then_inc(biases_s, 16)
                    sp.dma_start(bqkv_sb[:, :], bqkv.partition_broadcast(P)).then_inc(biases_s, 16)
                    sp.dma_start(w.bo[:, :], bo.partition_broadcast(P)).then_inc(biases_s, 16)

            def step(i, front=False, back=False, late=False, ahead=False, load=False):
                if front:
                    wait(sp, f.y_ready_s, i * TT)
                    sp.dma_start(f.x_res[:, :, :], tok_tiles(x, i)).then_inc(f.res_loaded_s, 16)
                if back:
                    wait(sp, roped_s, (i - 1) * TT)
                    sp.dma_start(rope_sb[:, :, :, :], rope[bass.ds((i - 1) * CH, CH), :].rearrange(
                        "(t p) (a d) -> p t a d", p=P, a=2)).then_inc(rope_loaded_s, 16)
                if late:
                    store_parts(i - 2)
                if load:
                    load_x(i + 2)
                if back:
                    sp.wait_ge(v_biased_s, i * TT)
                    sp.dma_start(tok_tiles(v_dram, i - 1), v_sb[:, :, :, :].rearrange("p t h w -> p t (h w)")).then_inc(v_out_s, 16)
                if front:
                    sp.wait_ge(f.y_ready_s, (i + 1) * TT)
                    sp.dma_start(tok_tiles(x2_dram, i), f.y[:, :, :]).then_inc(x2_out_s, 16)
            run(sp, step)
            sp.wait_ge(x2_out_s, CHUNKS * 16)
            sp.wait_ge(parts_out_s, CHUNKS * 16)
            sp.wait_ge(v_out_s, CHUNKS * 16)

        @block.gpsimd
        def _(pool):
            norm_constants(pool, f, consts_s)
            pool.memset(v_sb[:, :, :, :], 1.0).then_inc(consts_s, 1)

            def rope_tile(j, t):
                n = j * TT + t
                src = qk[:, t % 2, :, :]
                sin_low = rope_sb[:, t, 1:2, 0:HD // 2].to_broadcast([P, HQK, HD // 2])
                sin_high = rope_sb[:, t, 1:2, HD // 2:HD].to_broadcast([P, HQK, HD // 2])
                pool.wait_ge(qk_biased_s, n + 1)
                if t == 0:
                    pool.wait_ge(rope_loaded_s, (j + 1) * 16)
                wait(pool, roped_s, n)
                pool.tensor_tensor(qk_sin[:, :, 0:HD // 2], src[:, :, HD // 2:HD], sin_low, ALU.mult).then_inc(rope_step_s, 1)
                pool.tensor_tensor(qk_sin[:, :, HD // 2:HD], src[:, :, 0:HD // 2], sin_high, ALU.mult).then_inc(rope_step_s, 1)
                pool.wait_ge(rope_step_s, 2 * n + 2)
                pool.wait_ge(cos_s, n + 1)
                wait(pool, roped_t_s, n - 1)
                pool.tensor_tensor(qk_rot[:, t % 2, :], qk_cos[:, t % 2, :, :].rearrange("p h d -> p (h d)"),
                                   qk_sin[:, :, :].rearrange("p h d -> p (h d)"), ALU.add).then_inc(roped_s, 1)

            def second_part_late(j, t):
                pool.wait_ge(rest_s, j * TT + t + 1)
                pool.tensor_tensor(parts[:, 1, :, t * P:(t + 1) * P], rest[:, t % 2, :, :],
                                   w.consts[:, 3, 0:1].unsqueeze(2).to_broadcast([P, 4, P]), ALU.mult).then_inc(part1_late_s, 1)

            def last_part(j, t):
                n = j * TT + t
                if t < 2:
                    pool.wait_ge(part1_s, j * 2 + t + 1)
                else:
                    pool.wait_ge(part1_late_s, j * 2 + t - 1)
                if t == 0:
                    wait(pool, parts_out_s, j * 16)
                pool.tensor_tensor(parts[:, 2, :, t * P:(t + 1) * P], rest[:, t % 2, :, :],
                                   parts[:, 1, :, t * P:(t + 1) * P], ALU.subtract).then_inc(part2_s, 1)

            def step(i, front=False, back=False, late=False, ahead=False, load=False):
                if late:
                    for t in (TT - 2, TT - 1):
                        second_part_late(i - 2, t)
                        last_part(i - 2, t)
                if ahead:
                    norm_root(pool, f, f.ln1, i + 1)
                if back:
                    for t in range(TT):
                        rope_tile(i - 1, t)
                        if t >= 2:
                            last_part(i - 1, t - 2)
                if front:
                    norm_root(pool, f, ln2, i)
            run(pool, step)

        @block.tensor
        def _(pe):
            pe.wait_ge(ident_s, 16)

            def split(i, first, weight):
                if isinstance(i, int) and i == first:
                    pe.wait_ge(split_lo_s, weight + 1)

            def qkv_tile(j, t):
                n = j * TT + t
                if t == 0:
                    pe.wait_ge(x2_hi_s, (j + 1) * KD)
                    pe.wait_ge(x2_lo_s, (j + 1) * KD)
                wait(pe, qk_biased_s, n)
                wait(pe, v_biased_s, n)
                rows = slice(t * P, (t + 1) * P)
                product(pe, qk_bank, lambda c, k: x2nT[c][:, k, rows], lambda c, k: wqkv_sb[c][:, k, 0:2 * D], KD)
                product(pe, v_bank, lambda c, k: x2nT[c][:, k, rows], lambda c, k: wqkv_sb[c][:, k, 2 * D:3 * D],
                        KD).then_inc(qkv_s, 1)

            def turn_tile(j, t, ahead, i):
                n = j * TT + t
                if t < 2 and ahead:
                    pe.wait_ge(f.xn_lo_s, (i + 2) * KD)
                if t >= 2:
                    pe.wait_ge(rest_s, n - 1)
                pe.wait_ge(roped_s, n + 1)
                for c in range(4):
                    last = pe.transpose(f.tr[t % 2][:, c * P:(c + 1) * P], qk_rot[:, t % 2, c * P:(c + 1) * P], f.ident[:, :])
                last.then_inc(roped_t_s, 1)

            def turn_ahead(i, back):
                if back:
                    pe.wait_ge(x2_lo_s, i * KD)
                pe.wait_ge(f.ln1.normed_s, (i + 2) * TT)
                transpose_tokens(pe, f, f.xn).then_inc(f.xn_t_s, 1)

            def step(i, front=False, back=False, late=False, ahead=False, load=False):
                j = i - 1
                split(i, 0, W1)
                for b in range(FB):
                    if front:
                        pe_up(pe, f, i, b)
                    if front and b == 0:
                        if late:
                            pe.wait_ge(rest_s, (j - 1) * TT + 2)
                        pe_turn_logits(pe, f, i)
                    if front and b == 1:
                        pe.wait_ge(f.top_s, (i + 1) * TT)
                    if late and b < 2:
                        turn_tile(j - 1, TT - 2 + b, False, i)
                    if back and b == 4:
                        wait(pe, rest_s, j * TT)
                        pe.wait_ge(ln2.normed_s, (j + 1) * TT)
                        transpose_tokens(pe, f, x2n).then_inc(x2_t_s, 1)
                split(i, 0, W2)
                split(i, 1, WQKV)
                for t in range(TT):
                    if t == 2 and ahead:
                        turn_ahead(i, back)
                    if back:
                        qkv_tile(j, t)
                    if back and t >= 2:
                        turn_tile(j, t - 2, ahead, i)
                    if front and t == 3 and ahead:
                        pe_logits(pe, f, i + 1)
                    if front:
                        pe_down(pe, f, i, t)
                if ahead:
                    if not front:
                        split(i, -1, ROUTER)
                        pe.wait_ge(zeros_s, 2)
                        pe_logits(pe, f, i + 1)
            run(pe, step)

        @block.scalar
        def _(act):
            act.wait_ge(ident_s, 16)
            for part in w.router:
                act.activation(part[:, :, EXPERTS:P], w.ident[:, EXPERTS:P].unsqueeze(1).to_broadcast([P, KD, P - EXPERTS]),
                               ACT.Copy, scale=0.0).then_inc(zeros_s, 1)
            act_split(act, ROUTER)
            act_split(act, W1)
            act.wait_ge(biases_s, 4 * 16)

            def first_part(j, t):
                act.wait_ge(roped_t_s, j * TT + t + 1)
                if t == 0:
                    wait(act, parts_out_s, j * 16)
                act.activation(parts[:, 0, :, t * P:(t + 1) * P],
                               f.tr[t % 2].rearrange("p (c n) -> p c n", n=P), ACT.Copy).then_inc(part0_s, 1)

            def second_part(j, t):
                act.wait_ge(rest_s, j * TT + t + 1)
                act.activation(parts[:, 1, :, t * P:(t + 1) * P], rest[:, t % 2, :, :], ACT.Copy).then_inc(part1_s, 1)

            def step(i, front=False, back=False, late=False, ahead=False, load=False):
                j = i - 1
                for b in range(FB):
                    if front:
                        act_gelu(act, f, i, b)
                    if late and b < 2:
                        first_part(j - 1, TT - 2 + b)
                    if back and b == 4:
                        act.wait_ge(x2_t_s, j + 1)
                        wait(act, qkv_s, j * TT)
                        for k in range(KD):
                            take_hi(act, f, x2nT, k, x2_hi_s)
                if front:
                    act_router_exp(act, f, i)
                if ahead:
                    act.wait_ge(f.xn_t_s, i + 2)
                    for k in range(KD):
                        take_hi(act, f, f.xnT, k, f.xn_hi_s)
                if back:
                    first_part(j, 0)
                    second_part(j, 0)
                    first_part(j, 1)
                if ahead:
                    act_take_logits(act, f, i + 1)
                    act_fetch_gelu(act, f)
                if isinstance(i, int) and i == -1:
                    act_split(act, W2)
                if isinstance(i, int) and i == 0:
                    act_split(act, WQKV)
                    act_split(act, WO)
                if back:
                    second_part(j, 1)
            run(act, step)

        @block.vector
        def _(dve):
            def bias_tile(j, t):
                n = j * TT + t
                dve.wait_ge(qkv_s, n + 1)
                wait(dve, roped_s, n - 1)
                dve.tensor_tensor(qk[:, t % 2, :, :].rearrange("p h d -> p (h d)"), qk_bank,
                                  bqkv_sb[:, 0:2 * D], ALU.add).then_inc(qk_biased_s, 1)
                if t == 0:
                    wait(dve, v_out_s, j * 16)
                dve.tensor_tensor(v_sb[:, t, :, 0:HD], v_bank.rearrange("p (h d) -> p h d", d=HD),
                                  bqkv_sb[:, 2 * D:3 * D].rearrange("p (h d) -> p h d", d=HD),
                                  ALU.add).then_inc(v_biased_s, 1)
                if t == 0:
                    dve.wait_ge(rope_loaded_s, (j + 1) * 16)
                dve.wait_ge(qk_biased_s, n + 1)
                dve.tensor_tensor(qk_cos[:, t % 2, :, :], qk[:, t % 2, :, :],
                                  rope_sb[:, t, 0:1, :].to_broadcast([P, HQK, HD]), ALU.mult).then_inc(cos_s, 1)

            def rest_tile(j, t):
                n = j * TT + t
                dve.wait_ge(part0_s, n + 1)
                wait(dve, part2_s, n - 1)
                dve.tensor_tensor(rest[:, t % 2, :, :], f.tr[t % 2].rearrange("p (c n) -> p c n", n=P),
                                  parts[:, 0, :, t * P:(t + 1) * P], ALU.subtract).then_inc(rest_s, 1)

            def next_stats(i):
                dve.wait_ge(f.x_loaded_s, (i + 2) * 16)
                for t in range(TT):
                    norm_stats(dve, f.ln1, f.x_in, t)

            def next_apply(i, t):
                if t == 0:
                    wait(dve, f.xn_t_s, i + 1)
                norm_apply(dve, f.ln1, f.x_in, f.xn, i + 1, t)

            dve.wait_ge(consts_s, 5)

            def step(i, front=False, back=False, late=False, ahead=False, load=False):
                j = i - 1
                if front:
                    dve_router(dve, f, i)
                if isinstance(i, int) and i == 0:
                    dve_split(dve, W2)
                for b in range(5):
                    if front:
                        dve_gelu_lo(dve, f, i, b)
                    if late and b < 2:
                        rest_tile(j - 1, TT - 2 + b)
                    if back and b == 1:
                        wait(dve, x2_t_s, j)
                        for t in range(TT):
                            norm_apply(dve, ln2, f.y, x2n, j, t)
                    if ahead and b == 2:
                        next_stats(i)
                    if ahead and b == 3:
                        norm_moments(dve, f.ln1, i + 1)
                if isinstance(i, int) and i == -1:
                    dve_split(dve, ROUTER)
                    dve_split(dve, W1)
                    dve.wait_ge(biases_s, 4 * 16)
                if back:
                    wait(dve, qkv_s, j * TT)
                    for k in range(KD):
                        take_lo(dve, f, x2nT, k, j, x2_hi_s, x2_lo_s)
                for b in range(5, FB):
                    if front:
                        dve_gelu_lo(dve, f, i, b)
                if back:
                    bias_tile(j, 0)
                for t in range(TT):
                    if ahead:
                        next_apply(i, t)
                if front:
                    dve_gate(dve, f, i)
                    dve.wait_ge(f.res_loaded_s, (i + 1) * 16)
                    wait(dve, x2_out_s, i * 16)

                def tile(t):
                    if front:
                        dve_residual(dve, f, i, t, f.x_res)
                        dve.wait_ge(f.y_ready_s, i * TT + t + 1)
                        norm_stats(dve, ln2, f.y, t)
                tile(0)
                if back:
                    bias_tile(j, 1)
                tile(1)
                if ahead:
                    for k in range(KD):
                        take_lo(dve, f, f.xnT, k, i + 1, f.xn_hi_s, f.xn_lo_s)
                if back:
                    bias_tile(j, 2)
                tile(2)
                if back:
                    rest_tile(j, 0)
                    bias_tile(j, 3)
                    rest_tile(j, 1)
                tile(3)
                if front:
                    norm_moments(dve, ln2, i)
                if isinstance(i, int) and i == 0:
                    dve_split(dve, WQKV)
                    dve_split(dve, WO)
            run(dve, step)



def attention_phase(nc, phase, w, qk_dram, v_dram, ctx_dram):
    def sb(name, shape, dt=F32):
        return phase.enter_context(nc.sbuf_tensor("b_" + name, shape, dt))

    def sem(name):
        return phase.enter_context(nc.semaphore("b_" + name))

    SLOT = QUAD * SEQ
    ident_b = sb("ident_b", [P, P], BF16)
    q_stack = sb("q_stack", [STACK, RING * SLOT], BF16)
    k_stack = sb("k_stack", [STACK, RING * SLOT], BF16)
    v_sb = sb("v", [P, KB, QUAD, VW])
    probs = sb("probs", [P, 2, QUAD, CH])
    ctx_sb = sb("ctx_sb", [P, CH])
    PAIRS = QUAD * TT
    KP = SEQ // CH
    UNITS = PAIRS * KP
    maxes = sb("maxes", [P, PAIRS, KP])
    one = sb("one", [P, PAIRS])
    shift = sb("shift", [P, PAIRS])
    shift_rest = sb("shift_rest", [P, 2, PAIRS])
    shift_parts = sb("shift_parts", [P, P], BF16)
    shift_t = sb("shift_t", [PARTS * PAIRS, P], BF16)
    banks = phase.enter_context(nc.psum_tensor("b_banks", [P, 8, CH], F32))
    acc = banks[:, QUAD, :]
    NM = 3
    PASSES = GROUPS * QC
    TURN = 6
    NU = UNITS + 1
    AHEAD = 28

    ones_s = sem("ones")
    ident_s = sem("ident")
    one_s = sem("one")
    stack_s = sem("stack")
    v_s = [sem(f"v{p}") for p in range(4)]
    score_s = sem("score_ready")
    exp_s = sem("exped")
    pv_s = sem("pv_done")
    user_s = sem("max_bank_ready")
    freed_s = sem("max_bank_freed")
    shift_s = sem("shift_ready")
    split_s = sem("split_step")
    parts_s = sem("shift_parts")
    rows_s = sem("shift_rows")
    ctx_s = sem("ctx_ready")
    ctx_out_s = sem("ctx_out")
    LOADS = len(Q_PART) * 2 * 16
    ROWS = PARTS * QUAD * 16

    def bank_of(place):
        return banks[:, QUAD + 1 + place % NM, :]

    def done(n, place):
        if isinstance(n, int) and n == 0:
            return place + 1 if place < TURN else place
        if isinstance(n, int) and n == PASSES:
            return n * NU
        return n * NU + place

    def bank_free(n, place):
        first = isinstance(n, int) and n == 0
        before = [p for p in range(place) if p % NM == place % NM and not (first and p == TURN)]
        if isinstance(n, int) and n == PASSES:
            return n * NU - 1
        if before:
            return done(n, before[-1])
        return 0 if first else done(n - 1, max(p for p in range(NU) if p % NM == place % NM))

    def slot_of(n):
        return ((n // QC) % RING) * SLOT

    with nc.Block() as block:
        @block.sync
        def _(sp):
            def load_stacks(g):
                at = (g % RING) * SLOT
                if not (isinstance(g, int) and g < RING):
                    sp.wait_ge(score_s, (g - RING + 1) * QC * KB * 2)
                wait(sp, stack_s, g * LOADS)
                for r in range(len(Q_PART)):
                    for stack, part, which in ((q_stack, Q_PART[r], 0), (k_stack, K_PART[r], 1)):
                        rows = (g % QC) * (QUAD * HD) + (part * 2 + which) * D
                        src = qk_dram[bass.ds(g // QC, 1), bass.ds(rows, QUAD * HD), :].rearrange("b (j d) t -> d (b j) t", d=HD)
                        dst = stack[HD * r:HD * (r + 1), bass.ds(at, SLOT)].rearrange("p (j t) -> p j t", j=QUAD)
                        sp.dma_start(dst, src).then_inc(stack_s, 16)

            def load_v(g, piece):
                rows, cols = SEQ // 4, QUAD * VW
                src = v_dram[bass.ds((g // QC) * SEQ + piece * rows, rows), bass.ds((g % QC) * cols, cols)]
                sp.dma_start(v_sb[:, 4 * piece:4 * piece + 4, :, :].rearrange("p k h w -> p k (h w)"),
                             src.rearrange("(k p) n -> p k n", p=P)).then_inc(v_s[piece], 16)

            def store_rows(n):
                sp.wait_ge(freed_s, done(n + 1, TURN))
                at = slot_of(n) + (n % QC) * CH
                for c in range(PARTS):
                    for j in range(QUAD):
                        first = c * PAIRS + j * TT
                        sp.dma_start(q_stack[SHIFT_ROW + c:SHIFT_ROW + c + 1, bass.ds(at + j * SEQ, CH)],
                                     shift_t[first:first + TT, :]).then_inc(rows_s, 16)

            def store_ctx(m):
                sp.wait_ge(ctx_s, m + 1)
                dst = ctx_dram[bass.ds(m // QC, 1), :, bass.ds((m % QC) * CH, CH)].rearrange("g p t -> (g p) t")
                sp.dma_start(dst, ctx_sb[:, :]).then_inc(ctx_out_s, 16)

            load_stacks(0)
            for piece in range(4):
                load_v(0, piece)
            store_rows(0)

            def chunk(m, g, qc):
                last = isinstance(g, int) and g == GROUPS - 1
                if not last or qc < QC - 1:
                    store_rows(m + 1)
                if not (isinstance(m, int) and m == 0):
                    store_ctx(m - 1)
                if qc == QC - 1 and not last:
                    for piece in range(4):
                        sp.wait_ge(pv_s, m * KB + 4 * piece + 4)
                        load_v(g + 1, piece)

            for qc in range(QC):
                chunk(qc, 0, qc)
                if qc < 2:
                    load_stacks(1 + qc)
            with sp.Fori(1, GROUPS - 2) as g:
                load_stacks(g + 2)
                for qc in range(QC):
                    chunk(g * QC + qc, g, qc)
            for g in (GROUPS - 2, GROUPS - 1):
                for qc in range(QC):
                    chunk(g * QC + qc, g, qc)
            store_ctx(PASSES - 1)
            sp.wait_ge(ctx_out_s, PASSES * 16)

        @block.gpsimd
        def _(pool):
            pool.memset(one[:, :], 1.0).then_inc(one_s, 1)
            pool.wait_ge(one_s, 1)
            pool.memset(k_stack[SR:STACK, :], 1.0).then_inc(ones_s, 1)
            pool.wait_ge(ones_s, 1)

            with pool.Fori(0, PASSES) as n:
                pool.wait_ge(shift_s, n + 1)
                pool.tensor_tensor(shift_parts[:, 0 * PAIRS:1 * PAIRS], shift[:, :], one[:, :], ALU.mult).then_inc(split_s, 1)
                pool.wait_ge(split_s, 4 * n + 1)
                pool.tensor_tensor(shift_rest[:, 0, :], shift[:, :], shift_parts[:, 0 * PAIRS:1 * PAIRS], ALU.subtract).then_inc(split_s, 1)
                pool.wait_ge(split_s, 4 * n + 2)
                pool.tensor_tensor(shift_parts[:, 1 * PAIRS:2 * PAIRS], shift_rest[:, 0, :], one[:, :], ALU.mult).then_inc(split_s, 1)
                pool.wait_ge(split_s, 4 * n + 3)
                pool.tensor_tensor(shift_rest[:, 1, :], shift_rest[:, 0, :], shift_parts[:, 1 * PAIRS:2 * PAIRS], ALU.subtract).then_inc(split_s, 1)
                pool.wait_ge(split_s, 4 * n + 4)
                pool.tensor_tensor(shift_parts[:, 2 * PAIRS:3 * PAIRS], shift_rest[:, 1, :], one[:, :], ALU.mult).then_inc(parts_s, 1)

        @block.tensor
        def _(pe):
            pe.wait_ge(ident_s, 2)

            def unit(n, place, slot, at):
                pair, piece = divmod(place - (place > TURN), KP)
                j, tile = divmod(pair, TT)
                wait(pe, freed_s, bank_free(n, place))
                pe.matmul(bank_of(place), q_stack[0:SR, bass.ds(at + (j * SEQ + tile * P), P)],
                          k_stack[0:SR, bass.ds(slot + (j * SEQ + piece * CH), CH)],
                          start=True, stop=True).then_inc(user_s, 1)

            def turn(n):
                pe.wait_ge(parts_s, n)
                pe.wait_ge(freed_s, bank_free(n, TURN))
                pe.transpose(bank_of(TURN)[:, 0:P // 2].bitcast(BF16), shift_parts[:, :], ident_b[:, :]).then_inc(user_s, 1)

            def add_values(m, kb):
                if kb == 0:
                    wait(pe, ctx_s, m)
                if kb % 4 == 0:
                    pe.wait_ge(v_s[kb // 4], (m // QC + 1) * 16)
                for j in range(QUAD):
                    last = pe.matmul(acc[VW * j:VW * (j + 1), :], v_sb[:, kb, j, :], probs[:, kb % 2, j, :],
                                     start=(kb == 0), stop=(kb == KB - 1))
                last.then_inc(pv_s, 1)

            def places(n, first, end):
                if isinstance(n, int) and n == PASSES:
                    return [(n, TURN, None, None)] if first <= TURN < end else []
                slot, at = slot_of(n), slot_of(n) + (n % QC) * CH
                if not isinstance(n, int):
                    slot, at = pe.snap(slot), pe.snap(at)
                return [(n, place, slot, at) for place in range(first, end) if place != TURN or not (isinstance(n, int) and n == 0)]

            def users(todo, count):
                while count and todo:
                    n, place, slot, at = todo.pop(0)
                    if place == TURN:
                        turn(n)
                    else:
                        count -= 1
                        if place == 0:
                            pe.wait_ge(stack_s, (n // QC + 1) * LOADS)
                        unit(n, place, slot, at)

            def step(m):
                todo = []
                if not (isinstance(m, int) and m + 1 >= PASSES):
                    todo = places(m + 1, AHEAD, NU) + places(m + 2, 0, AHEAD)
                if isinstance(m, int) and m == 0:
                    pe.wait_ge(ones_s, 1)
                pe.wait_ge(rows_s, (m + 1) * ROWS)
                kslot = pe.snap(slot_of(m)) if not isinstance(m, int) else slot_of(m)
                qat = pe.snap(kslot + (m % QC) * CH) if not isinstance(m, int) else kslot + (m % QC) * CH

                def scores(kb, half):
                    for j in (2 * half, 2 * half + 1):
                        last = pe.matmul(banks[:, j, :], k_stack[:, bass.ds(kslot + (j * SEQ + kb * P), P)],
                                         q_stack[:, bass.ds(qat + j * SEQ, CH)], start=True, stop=True)
                    last.then_inc(score_s, 1)

                for kb in range(KB):
                    s = m * KB + kb
                    wait(pe, exp_s, 2 * s - 1)
                    scores(kb, 0)
                    users(todo, 1)
                    wait(pe, exp_s, 2 * s)
                    scores(kb, 1)
                    users(todo, 1)
                    if kb:
                        add_values(m, kb - 1)
                    elif not (isinstance(m, int) and m == 0):
                        add_values(m - 1, KB - 1)
                    users(todo, 2)

                users(todo, 1)
            users(places(0, 0, NU), NU)
            users(places(1, 0, AHEAD), NU)
            step(0)
            step(1)
            with pe.Fori(1, (PASSES - 2) // 2) as half:
                for part in range(2):
                    step(2 * half + part)
            step(PASSES - 2)
            step(PASSES - 1)
            pe.wait_ge(exp_s, 2 * PASSES * KB)
            add_values(PASSES - 1, KB - 1)

        @block.scalar
        def _(act):
            act.activation(ident_b[:, :], w.ident[:, :], ACT.Copy).then_inc(ident_s, 1)
            act.activation(shift_parts[:, PARTS * PAIRS:P], w.ident[:, PARTS * PAIRS:P], ACT.Copy, scale=0.0).then_inc(ident_s, 1)

            def take_context(m):
                act.wait_ge(pv_s, (m + 1) * KB)
                wait(act, ctx_out_s, m * 16)
                act.activation(ctx_sb[:, :], acc, ACT.Copy).then_inc(ctx_s, 1)

            def step(m):
                for kb in range(KB):
                    s = m * KB + kb
                    for half in range(2):
                        act.wait_ge(score_s, 2 * s + half + 1)
                        if half == 0:
                            wait(act, pv_s, s - 1)
                        act.activation(probs[:, kb % 2, 2 * half:2 * half + 2, :], banks[:, 2 * half:2 * half + 2, :],
                                       ACT.Exp, scale=SCORE_SCALE).then_inc(exp_s, 1)
                    if kb == 0 and not (isinstance(m, int) and m == 0):
                        take_context(m - 1)
            step(0)
            step(1)
            with act.Fori(1, PASSES // 2) as half:
                for part in range(2):
                    step(2 * half + part)
            take_context(PASSES - 1)

        @block.vector
        def _(dve):
            def turned(n):
                dve.wait_ge(user_s, done(n, TURN))
                wait(dve, rows_s, (n - 1) * ROWS)
                dve.tensor_copy(shift_t[:, :], bank_of(TURN)[0:PARTS * PAIRS, 0:P // 2].bitcast(BF16)).then_inc(freed_s, 1)

            def pass_max(n):
                wait(dve, shift_s, n)
                for place in range(NU):
                    if place == TURN:
                        if not (isinstance(n, int) and n == 0):
                            turned(n)
                        continue
                    pair, piece = divmod(place - (place > TURN), KP)
                    dve.wait_ge(user_s, done(n, place))
                    dve.reduce_max(maxes[:, pair, piece:piece + 1], bank_of(place), axis=X).then_inc(freed_s, 1)
                dve.wait_ge(freed_s, done(n, NU - 1))
                wait(dve, parts_s, n)
                dve.tensor_reduce(shift[:, :], maxes[:, :, :], X, ALU.max, negate=True).then_inc(shift_s, 1)
            pass_max(0)
            pass_max(1)
            with dve.Fori(1, PASSES // 2) as half:
                for part in range(2):
                    pass_max(2 * half + part)
            turned(PASSES)



def output_phase(nc, phase, w, x2_dram, ctx_dram, out):
    sb, sem = allocators(nc, phase, "c_")
    f = ffn_buffers(nc, phase, "c_", w)
    x2_sb = sb("x2", [P, TT, D])
    raw = sb("raw", [P, QUAD, CH])
    sum_rec = sb("sum_rec", [P, 2, HEADS])
    context = sb("context", [P, TT, D])
    contextT = split_pair(sb, "contextT", [P, KD, CH])
    projected = sb("projected", [P, TT, D])
    proj_banks = [f.banks[:, 6 + k, 0:D] for k in range(2)]

    raw_loaded_s = sem("raw_loaded")
    x2_loaded_s = sem("x2_loaded")
    raw_t_s = sem("raw_t")
    sum_rec_s = sem("sum_rec")
    context_s = sem("context_ready")
    context_t_s = sem("context_t")
    context_hi_s = sem("context_hi")
    context_lo_s = sem("context_lo")
    proj_s = sem("proj")
    proj_bias_s = sem("proj_bias")
    x3_s = sem("x3")
    out_s = sem("out")

    def run(eng, step):
        step(-1, ahead=True, load=True)
        step(0, front=True, ahead=True, load=True)
        with eng.Fori(1, CHUNKS - 2) as i:
            step(i, front=True, ahead=True, load=True)
        step(CHUNKS - 2, front=True, ahead=True)
        step(CHUNKS - 1, front=True)

    with nc.Block() as block:
        @block.sync
        def _(sp):
            def load_raw(j):
                wait(sp, raw_t_s, j * TT)
                sp.dma_start(raw[:, :, :], ctx_dram[bass.ds((j // QC) * QUAD, QUAD), :, bass.ds((j % QC) * CH, CH)].rearrange(
                    "g p t -> p g t")).then_inc(raw_loaded_s, 16)

            def load_x2(j):
                wait(sp, x3_s, j * TT)
                sp.dma_start(x2_sb[:, :, :], tok_tiles(x2_dram, j)).then_inc(x2_loaded_s, 16)

            def step(i, front=False, ahead=False, load=False):
                if load:
                    load_raw(i + 2)
                    load_x2(i + 2)
                if front:
                    sp.wait_ge(f.y_ready_s, (i + 1) * TT)
                    sp.dma_start(tok_tiles(out, i), f.y[:, :, :]).then_inc(out_s, 16)
            load_raw(0)
            load_x2(0)
            run(sp, step)
            sp.wait_ge(out_s, CHUNKS * 16)

        @block.gpsimd
        def _(pool):
            def step(i, front=False, ahead=False, load=False):
                if ahead:
                    norm_root(pool, f, f.ln1, i + 1)
                    wait(pool, f.y_ready_s, (i + 1) * TT)
                    pool.wait_ge(x3_s, (i + 2) * TT)
                    pool.tensor_tensor(f.x_res[:, :, :], f.x_in[:, :, :],
                                       f.consts[:, 3, :].unsqueeze(2).to_broadcast([P, TT, D]), ALU.mult).then_inc(f.res_copied_s, 1)
            run(pool, step)

        @block.tensor
        def _(pe):
            def turn_raw(j, t):
                if t == 0:
                    pe.wait_ge(raw_loaded_s, (j + 1) * 16)
                if t < 2:
                    wait(pe, f.xn_lo_s, j * KD)
                else:
                    pe.wait_ge(context_s, j * TT + t - 1)
                for g in range(QUAD):
                    last = pe.transpose(f.tr[t % 2][:, g * P:(g + 1) * P], raw[:, g, t * P:(t + 1) * P], f.ident[:, :])
                last.then_inc(raw_t_s, 1)

            def turn_context(j):
                pe.wait_ge(context_s, (j + 1) * TT)
                transpose_tokens(pe, f, context).then_inc(context_t_s, 1)

            def project(j, t):
                if t == 0:
                    pe.wait_ge(context_hi_s, (j + 1) * KD)
                    pe.wait_ge(context_lo_s, (j + 1) * KD)
                wait(pe, proj_bias_s, j * TT + t - 1)
                product(pe, proj_banks[t % 2], lambda c, k: contextT[c][:, k, t * P:(t + 1) * P],
                        lambda c, k: w.wo[c][:, k, :], KD).then_inc(proj_s, 1)

            def turn_ahead(j):
                pe.wait_ge(f.ln1.normed_s, (j + 1) * TT)
                transpose_tokens(pe, f, f.xn).then_inc(f.xn_t_s, 1)

            def step(i, front=False, ahead=False, load=False):
                j = i + 1
                for b in range(FB):
                    if front:
                        pe_up(pe, f, i, b)
                    if front and b == 0:
                        pe_turn_logits(pe, f, i)
                    if front and b == 1:
                        pe.wait_ge(f.top_s, (i + 1) * TT)
                    if ahead and b < TT:
                        turn_raw(j, b)
                    if ahead and b == TT + 1:
                        turn_context(j)
                if ahead:
                    for t in range(TT):
                        project(j, t)
                if front:
                    for t in range(3):
                        pe_down(pe, f, i, t)
                if ahead:
                    turn_ahead(j)
                if front:
                    pe_down(pe, f, i, 3)
                if ahead:
                    pe_logits(pe, f, j)
            run(pe, step)

        @block.scalar
        def _(act):
            def step(i, front=False, ahead=False, load=False):
                j = i + 1
                if front:
                    for b in range(TT + 2):
                        act_gelu(act, f, i, b)
                if ahead:
                    act.wait_ge(context_t_s, j + 1)
                    wait(act, proj_s, j * TT)
                    for k in range(KD):
                        take_hi(act, f, contextT, k, context_hi_s)
                if front:
                    for b in range(TT + 2, FB):
                        act_gelu(act, f, i, b)
                    act_router_exp(act, f, i)
                if ahead:
                    act.wait_ge(f.xn_t_s, j + 1)
                    for k in range(KD):
                        take_hi(act, f, f.xnT, k, f.xn_hi_s)
                    act_take_logits(act, f, j)
                    act_fetch_gelu(act, f)
            run(act, step)

        @block.vector
        def _(dve):
            def divide(j, t):
                n = j * TT + t
                raw_t = f.tr[t % 2].rearrange("p (h w) -> p h w", w=VW)
                dve.wait_ge(raw_t_s, n + 1)
                if t == 0:
                    wait(dve, context_t_s, j)
                dve.reciprocal(sum_rec[:, t % 2, :].unsqueeze(2), raw_t[:, :, HD:HD + 1]).then_inc(sum_rec_s, 1)
                dve.wait_ge(sum_rec_s, n + 1)
                dve.tensor_tensor(context[:, t, :].rearrange("p (h d) -> p h d", d=HD), raw_t[:, :, 0:HD],
                                  sum_rec[:, t % 2, :].unsqueeze(2).to_broadcast([P, HEADS, HD]), ALU.mult).then_inc(context_s, 1)

            def add_output(j, t):
                n = j * TT + t
                dve.wait_ge(proj_s, n + 1)
                if t == 0:
                    dve.wait_ge(x2_loaded_s, (j + 1) * 16)
                    wait(dve, f.res_copied_s, j)
                dve.tensor_tensor(projected[:, t, :], proj_banks[t % 2], w.bo[:, :], ALU.add).then_inc(proj_bias_s, 1)
                dve.wait_ge(proj_bias_s, n + 1)
                dve.tensor_tensor(f.x_in[:, t, :], projected[:, t, :], x2_sb[:, t, :], ALU.add).then_inc(x3_s, 1)

            def step(i, front=False, ahead=False, load=False):
                j = i + 1
                if front:
                    dve_router(dve, f, i)
                for b in range(TT + 2):
                    if front:
                        dve_gelu_lo(dve, f, i, b)
                    if ahead and b < TT:
                        divide(j, b)
                if ahead:
                    wait(dve, proj_s, j * TT)
                    for k in range(KD):
                        take_lo(dve, f, contextT, k, j, context_hi_s, context_lo_s)
                for t in range(TT):
                    if front and t < 2:
                        dve_gelu_lo(dve, f, i, FB - 2 + t)
                    if ahead:
                        add_output(j, t)
                        dve.wait_ge(x3_s, j * TT + t + 1)
                        norm_stats(dve, f.ln1, f.x_in, t)
                if ahead:
                    norm_moments(dve, f.ln1, j)
                if front:
                    dve_gate(dve, f, i)
                    dve.wait_ge(f.res_copied_s, i + 1)
                    wait(dve, out_s, i * 16)
                    for t in range(2):
                        dve_residual(dve, f, i, t, f.x_res)
                if ahead:
                    wait(dve, f.xn_t_s, j)
                    for t in range(TT):
                        norm_apply(dve, f.ln1, f.x_in, f.xn, j, t)
                if front:
                    dve_residual(dve, f, i, 2, f.x_res)
                if ahead:
                    for k in range(KD):
                        take_lo(dve, f, f.xnT, k, j, f.xn_hi_s, f.xn_lo_s)
                if front:
                    dve_residual(dve, f, i, 3, f.x_res)
            run(dve, step)


def rope_table():
    import numpy as np

    half = HD // 2
    inv = (np.float32(1.0) / np.power(np.float32(10000.0), np.arange(half, dtype=np.float32) / np.float32(half))).astype(np.float32)
    angle = np.outer(np.arange(SEQ, dtype=np.float32), inv).astype(np.float32)
    cos, sin = np.cos(angle), np.sin(angle)
    table = np.concatenate([cos, cos, -sin, sin], axis=1).astype(np.float32)
    return np.tile(table, (BATCH, 1))


def kernel(**inputs):
    import numpy as np
    from concourse import bacc
    from concourse.bass_utils import run_bass_kernel_spmd

    a = {name: np.asarray(value) for name, value in inputs.items()}
    arrays = {
        "x": a["L0_attn_x"].reshape(TOKENS, D),
        "wqkv": np.concatenate([a["L0_attn_Wq"].T, a["L0_attn_Wk"].T, a["L0_attn_Wv"].T], axis=1),
        "bqkv": np.concatenate([a["L0_attn_bq"], a["L0_attn_bk"], a["L0_attn_bv"]]).reshape(1, 3 * D),
        "wo": a["L0_attn_Wo"].T,
        "bo": a["L0_attn_bo"].reshape(1, D),
        "router": a["L0_ffn_router_w"],
        "w1": a["L0_ffn_w1"],
        "b1": a["L0_ffn_b1"].reshape(FB, P).T,
        "w2": a["L0_ffn_w2"],
        "b2": a["L0_ffn_b2"].reshape(1, D),
        "rope": rope_table(),
        "ident": np.eye(P, dtype=np.float32),
    }
    arrays = {name: np.ascontiguousarray(value) for name, value in arrays.items()}
    nc = bacc.Bacc("TRN2", target_bir_lowering=False, num_devices=1)
    ins = [nc.dram_tensor(name, v.shape, mybir.dt.from_np(v.dtype), kind="ExternalInput").ap() for name, v in arrays.items()]
    out = nc.dram_tensor("out", (TOKENS, D), F32, kind="ExternalOutput").ap()
    build(nc, *ins, out)
    got = run_bass_kernel_spmd(nc, [arrays], core_ids=[0])
    return got.results[0]["out"].reshape(BATCH, SEQ, D)
```
